# Optimizing a Trainium2 kernel written in Bass

```python
import numpy as np
import jax
import jax.numpy as jnp

def _softmax(x, axis=-1):
    return jax.nn.softmax(x, axis=axis)

def _gelu(x):
    return jax.nn.gelu(x, approximate=True)

def _silu(x):
    return jax.nn.silu(x)

def _sigmoid(x):
    return jax.nn.sigmoid(x)

def _layernorm(x, axis=-1, eps=1e-05):
    m = jnp.mean(x, axis=axis, keepdims=True)
    v = jnp.var(x, axis=axis, keepdims=True)
    return (x - m) / jnp.sqrt(v + eps)

def _scatter_add(tgt, idx, src, axis=0):
    return tgt.at[idx].add(src)

def _segment_sum(src, seg, n):
    return jax.ops.segment_sum(src, seg, n)
kernel_name = 'mk_gnn_ffn_d1_gnn_r8_ee07f5'

def setup_inputs(seed: int=0):
    np.random.seed(seed)
    _w = jnp.asarray

    def _rec_inputs():
        import jax
        import jax.numpy as jnp
        _gk = jax.random.key(seed)
        x = -0.0002117 + 1 * jax.random.normal(jax.random.fold_in(_gk, 1), (1250, 512), jnp.float32)
        src = jax.random.randint(jax.random.fold_in(_gk, 2), (20000,), 0, 1250, jnp.int32)
        dst = jax.random.randint(jax.random.fold_in(_gk, 3), (20000,), 0, 1250, jnp.int32)
        _o = jnp.argsort(dst, stable=True)
        src = src[_o]
        dst = dst[_o]
        edge_type_4 = jax.random.randint(jax.random.fold_in(_gk, 12), (20000,), 0, 4, jnp.int32)
        edge_weight = jax.random.uniform(jax.random.fold_in(_gk, 13), (20000,), jnp.float32, 0.0, 0.999995)
        return (x, src, dst, edge_type_4, edge_weight)
    x, src, dst, edge_type_4, edge_weight = _rec_inputs()

    def _L0_gnn_setup():
        import jax, jax.numpy as jnp
        import numpy as np
        DIM = 512
        NUM_REL = 4
        N_NODES = 6250
        N_EDGES = 20000

        def _layer_norm(x, g, b, eps=1e-05):
            mu = jnp.mean(x, axis=-1, keepdims=True)
            var = jnp.mean((x - mu) ** 2, axis=-1, keepdims=True)
            return (x - mu) * jax.lax.rsqrt(var + eps) * g + b
        key = jax.random.key(seed)
        ks = jax.random.split(key, 16)
        s = 1.0 / np.sqrt(DIM)
        inp = {'x': jax.random.normal(ks[0], (N_NODES, DIM), jnp.float32), 'edge_index': jax.random.randint(ks[1], (2, N_EDGES), 0, N_NODES, jnp.int32), 'edge_type': jax.random.randint(ks[2], (N_EDGES,), 0, NUM_REL, jnp.int32), 'edge_weight': jax.random.uniform(ks[3], (N_EDGES,), jnp.float32), 'W_self': jax.random.uniform(ks[4], (DIM, DIM), jnp.float32, -s, s), 'b_self': jnp.zeros((DIM,), jnp.float32), 'W_rel': jax.random.uniform(ks[5], (NUM_REL, DIM, DIM), jnp.float32, -s, s), 'b_rel': jnp.zeros((NUM_REL, DIM), jnp.float32), 'ln1_g': jnp.ones((DIM,), jnp.float32), 'ln1_b': jnp.zeros((DIM,), jnp.float32), 'ln2_g': jnp.ones((DIM,), jnp.float32), 'ln2_b': jnp.zeros((DIM,), jnp.float32), 'W_ffn1': jax.random.uniform(ks[6], (DIM, 2 * DIM), jnp.float32, -s, s), 'b_ffn1': jnp.zeros((2 * DIM,), jnp.float32), 'W_ffn2': jax.random.uniform(ks[7], (2 * DIM, DIM), jnp.float32, -1.0 / np.sqrt(2 * DIM), 1.0 / np.sqrt(2 * DIM)), 'b_ffn2': jnp.zeros((DIM,), jnp.float32)}
        return inp
    _L0_gnn_all = _L0_gnn_setup()
    _L0_gnn_in = {k: v for k, v in _L0_gnn_all.items() if k in ('W_self', 'b_self', 'W_rel', 'b_rel', 'ln1_g', 'ln1_b', 'ln2_g', 'ln2_b', 'W_ffn1', 'b_ffn1', 'W_ffn2', 'b_ffn2')}
    del _L0_gnn_all

    def _L0_ffn_setup():
        import jax, jax.numpy as jnp
        import numpy as np
        from jax import lax
        N_EXPERTS = 16
        TOP_K = 2
        D_MODEL = 512
        D_FF = 256
        key = jax.random.key(seed)
        ks = jax.random.split(key, 7)
        s_in = 1.0 / np.sqrt(D_MODEL)
        s_ff = 1.0 / np.sqrt(D_FF)
        x = jax.random.normal(ks[0], (2, 256, D_MODEL), dtype=jnp.float32)
        router_w = jax.random.uniform(ks[1], (N_EXPERTS, D_MODEL), jnp.float32, -s_in, s_in)
        router_b = jax.random.uniform(ks[2], (N_EXPERTS,), jnp.float32, -s_in, s_in)
        w1 = jax.random.uniform(ks[3], (N_EXPERTS, D_FF, D_MODEL), jnp.float32, -s_in, s_in)
        b1 = jax.random.uniform(ks[4], (N_EXPERTS, D_FF), jnp.float32, -s_in, s_in)
        w2 = jax.random.uniform(ks[5], (N_EXPERTS, D_MODEL, D_FF), jnp.float32, -s_ff, s_ff)
        b2 = jax.random.uniform(ks[6], (N_EXPERTS, D_MODEL), jnp.float32, -s_ff, s_ff)
        return {'x': x, 'router_w': router_w, 'router_b': router_b, 'w1': w1, 'b1': b1, 'w2': w2, 'b2': b2}
    _L0_ffn_all = _L0_ffn_setup()
    _L0_ffn_in = {k: v for k, v in _L0_ffn_all.items() if k in ('router_w', 'router_b', 'w1', 'b1', 'w2', 'b2')}
    del _L0_ffn_all
    return {'x': x, 'src': src, 'dst': dst, 'edge_type_4': edge_type_4, 'edge_weight': edge_weight, 'L0_gnn_W_self': _L0_gnn_in['W_self'], 'L0_gnn_b_self': _L0_gnn_in['b_self'], 'L0_gnn_W_rel': _L0_gnn_in['W_rel'], 'L0_gnn_b_rel': _L0_gnn_in['b_rel'], 'L0_gnn_ln1_g': _L0_gnn_in['ln1_g'], 'L0_gnn_ln1_b': _L0_gnn_in['ln1_b'], 'L0_gnn_ln2_g': _L0_gnn_in['ln2_g'], 'L0_gnn_ln2_b': _L0_gnn_in['ln2_b'], 'L0_gnn_W_ffn1': _L0_gnn_in['W_ffn1'], 'L0_gnn_b_ffn1': _L0_gnn_in['b_ffn1'], 'L0_gnn_W_ffn2': _L0_gnn_in['W_ffn2'], 'L0_gnn_b_ffn2': _L0_gnn_in['b_ffn2'], 'L0_ffn_router_w': _L0_ffn_in['router_w'], 'L0_ffn_router_b': _L0_ffn_in['router_b'], 'L0_ffn_w1': _L0_ffn_in['w1'], 'L0_ffn_b1': _L0_ffn_in['b1'], 'L0_ffn_w2': _L0_ffn_in['w2'], 'L0_ffn_b2': _L0_ffn_in['b2']}

def reference(x, src, dst, edge_type_4, edge_weight, L0_gnn_W_self, L0_gnn_b_self, L0_gnn_W_rel, L0_gnn_b_rel, L0_gnn_ln1_g, L0_gnn_ln1_b, L0_gnn_ln2_g, L0_gnn_ln2_b, L0_gnn_W_ffn1, L0_gnn_b_ffn1, L0_gnn_W_ffn2, L0_gnn_b_ffn2, L0_ffn_router_w, L0_ffn_router_b, L0_ffn_w1, L0_ffn_b1, L0_ffn_w2, L0_ffn_b2):
    import jax
    import jax.numpy as jnp

    def _L0_gnn_ref(x, edge_index, edge_type, edge_weight, W_self, b_self, W_rel, b_rel, ln1_g, ln1_b, ln2_g, ln2_b, W_ffn1, b_ffn1, W_ffn2, b_ffn2):
        import jax, jax.numpy as jnp
        import numpy as np
        DIM = 512
        NUM_REL = 4
        N_NODES = 6250
        N_EDGES = 20000

        def _layer_norm(x, g, b, eps=1e-05):
            mu = jnp.mean(x, axis=-1, keepdims=True)
            var = jnp.mean((x - mu) ** 2, axis=-1, keepdims=True)
            return (x - mu) * jax.lax.rsqrt(var + eps) * g + b
        n = x.shape[0]
        src, dst = (edge_index[0], edge_index[1])
        xs = x[src]
        total_msg = jnp.zeros_like(xs)
        for r in range(NUM_REL):
            w_r = jnp.where(edge_type == r, edge_weight, 0.0)
            total_msg = total_msg + (xs @ W_rel[r] + b_rel[r]) * w_r[:, None]
        agg = jax.ops.segment_sum(total_msg, dst, num_segments=n)
        deg = jax.ops.segment_sum(edge_weight, dst, num_segments=n)
        agg = agg / jnp.maximum(deg, 1.0)[:, None]
        h = x @ W_self + b_self + agg
        x1 = _layer_norm(x + h, ln1_g, ln1_b)
        ffn = jax.nn.gelu(x1 @ W_ffn1 + b_ffn1, approximate=False) @ W_ffn2 + b_ffn2
        out = _layer_norm(x1 + ffn, ln2_g, ln2_b)
        return out

    def _L0_ffn_ref(x, router_w, router_b, w1, b1, w2, b2):
        import jax, jax.numpy as jnp
        import numpy as np
        from jax import lax
        N_EXPERTS = 16
        TOP_K = 2
        D_MODEL = 512
        D_FF = 256
        B, S, D = x.shape
        xt = x.reshape(-1, D)
        logits = xt @ router_w.T + router_b
        probs = jax.nn.softmax(logits, axis=-1)
        topk_p, topk_i = lax.top_k(probs, TOP_K)
        onehot = jax.nn.one_hot(topk_i, N_EXPERTS, dtype=probs.dtype)
        gates = jnp.sum(onehot * topk_p[..., None], axis=1)

        def expert_step(acc, packed):
            w1e, b1e, w2e, b2e, ge = packed
            h = jax.nn.gelu(xt @ w1e.T + b1e, approximate=False)
            y = h @ w2e.T + b2e
            return (acc + y * ge[:, None], None)
        out, _ = lax.scan(expert_step, jnp.zeros_like(xt), (w1, b1, w2, b2, gates.T))
        return out.reshape(B, S, D)
    edge_index = jnp.stack([src, dst])
    x = x + _L0_gnn_ref(_layernorm(x, axis=-1), edge_index, edge_type_4, edge_weight, L0_gnn_W_self, L0_gnn_b_self, L0_gnn_W_rel, L0_gnn_b_rel, L0_gnn_ln1_g, L0_gnn_ln1_b, L0_gnn_ln2_g, L0_gnn_ln2_b, L0_gnn_W_ffn1, L0_gnn_b_ffn1, L0_gnn_W_ffn2, L0_gnn_b_ffn2)
    x = x + _L0_ffn_ref(_layernorm(x, axis=-1)[None], L0_ffn_router_w, L0_ffn_router_b, L0_ffn_w1, L0_ffn_b1, L0_ffn_w2, L0_ffn_b2)[0]
    return x

_drawn_inputs = setup_inputs


def setup_inputs(seed=0):
    import zlib

    import numpy as np

    out = dict(_drawn_inputs(seed))
    spreads = {'L0_gnn_b_self': (0.0, 0.1),
     'L0_gnn_b_rel': (0.0, 0.312),
     'L0_gnn_ln1_g': (1.0, 0.2),
     'L0_gnn_ln1_b': (0.0, 0.1),
     'L0_gnn_ln2_g': (1.0, 0.2),
     'L0_gnn_ln2_b': (0.0, 0.1),
     'L0_gnn_b_ffn1': (0.0, 0.434),
     'L0_gnn_b_ffn2': (0.0, 0.1)}
    factors = {'L0_ffn_router_w': 2.698, 'L0_ffn_router_b': 22.318, 'L0_ffn_b1': 26.468, 'L0_ffn_b2': 8.0}
    for name, (base, spread) in spreads.items():
        noise = np.random.default_rng([zlib.crc32(name.encode()), seed]).standard_normal(out[name].shape)
        drawn = base * np.exp(spread * noise) if base else spread * noise
        out[name] = jnp.asarray(drawn.astype(out[name].dtype))
    for name, factor in factors.items():
        out[name] = (out[name] * factor).astype(out[name].dtype)
    return out
```

```python
from contextlib import ExitStack

import concourse.bass as bass
from concourse import mybir

F32 = mybir.dt.float32
BF16 = mybir.dt.bfloat16
I32 = mybir.dt.int32
U32 = mybir.dt.uint32
ALU = mybir.AluOpType
ACT = mybir.ActivationFunctionType
AX = mybir.AxisListType
ds = bass.ds

P = 128
D = 512
KD = D // P
NODES = 1250
NT = -(-NODES // P)
NP = NT * P
EDGES = 20000
EC = -(-EDGES // P)
ECP = EC + 1
REL = 4
FF = 1024
KF = FF // P
EPS = 1e-5

GROUP = 4
RING = 3 * GROUP
FAST = -(-(EC + NT - 1) // RING)
ALL = -(-EC * NT // RING)
PAIRS = (ALL + 1) * RING
PIECE = PAIRS // 4
AW = D + 2
BLOCK_SHIFT = 7

EXPERTS = 16
EF = 256
KE = EF // P
SLOT_TILES = (2 * NP + EXPERTS * (P - 1)) // P
EW = KD * EF + KE * D + KE
MR = 5
assert SLOT_TILES % MR == 0 and PAIRS % 4 == 0 and NT % 2 == 0

V_SELF, V_REL, V_G1, V_B1, V_G2, V_B2, V_F2, NV = 0, 1, 5, 6, 7, 8, 9, 10


def several(nc, engine, table, most):
    _, values = nc.values_load_multi_w_load_instructions(
        table, engines=(engine,), min_val=0, max_val=most,
        skip_runtime_bounds_check_because="the table is worked out from sums that stay within the bounds")
    return values


class Turn:

    def __init__(self, eng, sem, first, step):
        self.eng, self.sem, self.step = eng, sem, step
        self.reg = eng.alloc_register()
        eng.reg_mov(self.reg, first)

    def wait(self):
        self.eng.wait_ge(self.sem, self.reg)
        self.eng.reg_add(self.reg, self.reg, self.step)


class Steps:

    def __init__(self, sem):
        self.sem, self.n, self.at, self.per = sem, 0, None, 0

    def loop(self, it, per):
        self.at, self.per, self.first = it, per, self.n

    def end(self, trips):
        assert self.n - self.first == self.per, (self.n - self.first, self.per)
        self.n = self.first + self.per * trips
        self.at = None

    def did(self, ins):
        ins.then_inc(self.sem, 1)
        self.n += 1

    def now(self):
        return self.n if self.at is None else self.at * self.per + self.n


def program(nc, x, src, dst, typ, wgt, w_self, w_rel, vecs, w1, w2, bf1, rwT, rb, experts, eb2, out):
    ctx = ExitStack()
    with ctx:
        def sb(name, shape, dt=F32):
            return ctx.enter_context(nc.sbuf_tensor(name, shape, dt))

        def sem(name):
            return ctx.enter_context(nc.semaphore(name))

        msg = nc.dram_tensor("msg", (REL * NP, D), F32, kind="Internal").ap()
        xslot = nc.dram_tensor("xslot", (SLOT_TILES * P, D), F32, kind="Internal").ap()
        yslot = nc.dram_tensor("yslot", (SLOT_TILES * P, D), F32, kind="Internal").ap()

        ident = sb("ident", [P, P])
        ones = sb("ones", [P, P])
        tri_incl = sb("tri_incl", [P, P])
        ones_bf = sb("ones_bf", [P, P], BF16)
        tri_bf = sb("tri_bf", [P, P], BF16)
        num = sb("num", [P, PAIRS])
        vec = sb("vec", [P, NV, D])
        wreg = sb("wreg", [P, MR * EW])
        x_res = sb("x_res", [P, NT, D])
        work = sb("work", [P, NT, D])
        agg = sb("agg", [P, NT * AW])
        greg = sb("greg", [P, RING * D])
        treg = sb("treg", [P, NT * D + 5 * D])
        sel = sb("sel", [P, RING, P])
        src_i, dst_i, typ_i, blk_i = (sb(n, [P, ECP], I32) for n in ("src_i", "dst_i", "typ_i", "blk_i"))
        w_e = sb("w_e", [P, ECP])
        erow = sb("erow", [P, ECP])
        blk_f = sb("blk_f", [P, ECP])
        dstw = sb("dstw", [P, ECP, 2])
        dw = sb("dw", [P, RING, 2])
        row_i = sb("row_i", [P, RING], I32)
        lohi = sb("lohi", [P, 2, 2])
        npc = sb("npc", [P, 2])
        s_end = sb("s_end", [P, 2])
        s_beg = sb("s_beg", [P, 2])
        a_off = sb("a_off", [P, 2])
        npair = sb("npair", [1, 2], I32)
        steps = sb("steps", [33, PAIRS], I32)
        ctab = steps[0:1, :]
        btab = steps[32:33, :]
        st = sb("st", [P, NT, 6])
        mv = sb("mv", [P, NT, 2])
        var = sb("var", [P, NT])
        rs = sb("rs", [P, NT])
        mhalf = sb("mhalf", [P, NT])
        sm = sb("sm", [P, 2, 8])
        bf1_s = sb("bf1_s", [P, KF])
        rw_s = sb("rw_s", [P, KD, EXPERTS])
        rb_s = sb("rb_s", [P, EXPERTS])
        lg = sb("lg", [P, NT, EXPERTS])
        eb2_s = sb("eb2_s", [EXPERTS, D])
        ps = ctx.enter_context(nc.psum_tensor("ps", [P, 8 * D], F32))

        def flat(ap):
            return ap.rearrange("p a b -> p (a b)")

        def flat_rows(ap):
            return ap.rearrange("a p n -> (a p) n")

        def bank(i, a=0, n=D):
            return ps[:, i * D + a:i * D + a + n]

        ws_v = wreg[:, 0:KD * D].rearrange("p (k n) -> p k n", k=KD)
        wr_v = wreg[:, KD * D:5 * KD * D]
        w1_v = wreg[:, 0:KD * FF].rearrange("p (k n) -> p k n", k=KD)
        w2_v = wreg[:, KD * FF:KD * FF + KF * D].rearrange("p (k n) -> p k n", k=KF)
        ew_v = wreg[:, 0:MR * EW].rearrange("p (u n) -> p u n", u=MR)
        xT = treg[:, 0:NT * D].rearrange("p (t k n) -> p t k n", t=NT, k=KD)
        stage = treg[:, NT * D:].rearrange("p (u n) -> p u n", u=5)
        gath = greg[:, :].rearrange("p (u n) -> p u n", u=RING)
        HB = PAIRS // 2

        def bfrow(i):
            return greg[:, i * HB:(i + 1) * HB].bitcast(BF16)

        le_end = [bfrow(0), bfrow(1)]
        in_blk = [bfrow(2), bfrow(3)]
        le_beg = [bfrow(4), bfrow(5)]
        h1 = greg[:, 0:2 * D].rearrange("p (s n) -> p s n", s=2)
        x1 = greg[:, 2 * D:4 * D].rearrange("p (s n) -> p s n", s=2)
        hT = greg[:, 6 * D:10 * D].rearrange("p (k n) -> p k n", k=KF)
        tmp = greg[:, 10 * D:12 * D].rearrange("p (s n) -> p s n", s=2)
        x1T = treg[:, 0:2 * D].rearrange("p (k s n) -> p k s n", k=KD, s=2)
        xm = treg[:, 2 * D:4 * D].rearrange("p (s n) -> p s n", s=2)
        xmT = treg[:, 4 * D:6 * D].rearrange("p (s k n) -> p s k n", s=2, k=KD)
        y1 = treg[:, 6 * D:8 * D].rearrange("p (s n) -> p s n", s=2)
        R = NT * EXPERTS
        xs = greg[:, 0:MR * D].rearrange("p (u n) -> p u n", u=MR)
        ys = greg[:, MR * D:2 * MR * D].rearrange("p (u n) -> p u n", u=MR)
        SCR = (0, 1, 2, 0, 1)
        xsT = treg[:, 0:3 * D].rearrange("p (s k n) -> p s k n", s=3, k=KD)
        ehT = treg[:, 3 * D:3 * D + 3 * EF].rearrange("p (s k n) -> p s k n", s=3, k=KE)
        yg = greg[:, 0:8 * D].rearrange("p (u c n) -> p u c n", u=4, c=2)

        rt = treg[:, 12 * D:15 * D]

        def rslot(i, n=R):
            return rt[:, i * R:i * R + n].rearrange("p (t e) -> p t e", e=EXPERTS) if n == R else rt[:, i * R:i * R + n]

        e1 = rslot(0)
        e2 = rslot(1)
        rank = rslot(2)
        prod = rslot(3)
        probs = rslot(4)
        oh_bf = rt[:, 5 * R:5 * R + R // 2].bitcast(BF16)
        gate_all = rslot(6)
        cum = rt[:, 7 * R:7 * R + R + EXPERTS].rearrange("p (t e) -> p t e", e=EXPERTS)
        m8 = sb("m8", [P, NT, 8])
        i8 = sb("i8", [P, NT, 8], U32)
        idx_f = sb("idx_f", [P, NT, 2])
        pos_f = sb("pos_f", [P, NT, 2])
        pos_i = sb("pos_i", [P, NT * 2], I32)
        row16 = sb("row16", [P, 8, EXPERTS])
        cnt_i = sb("cnt_i", [P, EXPERTS], I32)
        tcmp = treg[0:1, 8 * D:8 * D + (SLOT_TILES + 1) * EXPERTS].rearrange("p (t e) -> p t e", e=EXPERTS)
        texp_f = sb("texp_f", [1, SLOT_TILES + 1])
        texp = sb("texp", [1, SLOT_TILES + 1], I32)
        gT = agg[0:EXPERTS, 0:NT * P].rearrange("p (t n) -> p t n", t=NT)

        s_x = sem("x_in")
        s_edge = sem("edges_in")
        s_vec = sem("vecs_in")
        s_wself = sem("w_self_in")
        s_wrel = sem("w_rel_in")
        s_cst = sem("constants")
        s_dve = sem("dve_step")
        s_blk = sem("edge_tiles")
        s_blkT = sem("edge_tiles_transposed")
        s_npc = sem("pairs_per_chunk")
        s_pre = sem("pair_prefix")
        s_off = sem("pair_offsets")
        s_pool = sem("pool_step")
        s_mask = sem("step_masks")
        s_tabp = sem("table_piece")
        s_tabc = sem("table_copied")
        s_var = sem("variances")
        s_rs = sem("one_over_sigma")
        s_xn = sem("x_normed")
        s_xnT = sem("x_transposed")
        s_xTc = sem("x_transposed_in_sbuf")
        s_sb = sem("b_self_added")
        s_prod = sem("product_ready")
        s_evac = sem("product_taken")
        s_tab = [sem(f"msg_rows_out{u}") for u in range(5)]
        s_zero = sem("xslot_cleared")
        s_etab = sem("edge_table")
        s_idx = sem("step_indices")
        s_gath = [sem(f"gathered{u}") for u in range(RING)]
        s_sel = sem("one_hot_ready")
        s_mm = sem("step_product")
        s_sums = sem("sums_written")
        s_aggd = sem("aggregated")
        s_ffw = sem("ffn_weights_in")
        c_dve = sem("node_dve_step")
        c_var = sem("node_variance")
        c_rs = sem("node_one_over_sigma")
        c_pool = sem("node_pool_step")
        c_x1 = sem("x1_ready")
        c_x1T = sem("x1_transposed")
        c_x1Tc = sem("x1_transposed_in_sbuf")
        c_x1b = sem("x1_plus_bias")
        c_h = sem("hidden_product")
        c_g = sem("hidden_gelu")
        c_f = sem("ffn_product")
        c_ft = sem("ffn_taken")
        c_xm = sem("expert_input_ready")
        c_xmT = sem("expert_input_transposed")
        c_xmTc = sem("expert_input_T_in_sbuf")
        c_lg = sem("logits_product")
        c_lgt = sem("logits_taken")
        d_dve = sem("route_dve_step")
        d_lg0 = sem("logits_centred")
        d_ex = sem("logits_exp")
        d_oh = sem("one_hots")
        d_cnt = sem("counts_product")
        d_tab = sem("expert_table")
        d_pos = sem("slots_ready")
        d_sc = sem("rows_scattered")
        d_gall = sem("gates_ready")
        d_gT = sem("gates_transposed")
        d_gTc = sem("gates_T_in_sbuf")
        d_b2 = sem("bias_product")
        d_b2t = sem("bias_taken")
        e_w = [sem(f"expert_weights_in{u}") for u in range(MR)]
        e_x = [sem(f"slot_rows_in{u}") for u in range(MR)]
        e_xT = sem("slot_rows_transposed")
        e_xTc = sem("slot_rows_T_in_sbuf")
        e_h = sem("expert_hidden_product")
        e_g = sem("expert_hidden_gelu")
        e_y = sem("expert_product")
        e_yt = sem("expert_product_taken")
        e_out = [sem(f"slot_rows_out{u}") for u in range(MR)]
        f_g = [sem(f"results_gathered{u}") for u in range(4)]
        f_dve = sem("combine_step")
        f_done = sem("tile_combined")
        f_out = sem("out_written")

        msg_t = msg.rearrange("(r t p) d -> (r t) p d", r=REL, p=P)
        xslot_t = xslot.rearrange("(t p) d -> t p d", p=P)
        yslot_t = yslot.rearrange("(t p) d -> t p d", p=P)

        block = ctx.enter_context(nc.Block())

        @block.sync
        def _(sp):
            for a, b in ((dst_i, dst), (src_i, src), (typ_i, typ)):
                sp.dma_start(a[:, :], b).then_inc(s_edge, 16)
            sp.dma_start(w_e[:, :], wgt).then_inc(s_edge, 16)
            sp.dma_start(x_res[:, :, :], x.rearrange("(t p) d -> p t d", p=P)).then_inc(s_x, 16)
            sp.dma_start(ws_v, w_self.rearrange("(k p) n -> p k n", p=P)).then_inc(s_wself, 16)
            sp.wait_ge(s_wself, 16)
            for r in range(REL):
                sp.dma_start(wr_v[:, r * KD * D:(r + 1) * KD * D].rearrange("p (k n) -> p k n", k=KD),
                             w_rel[r].rearrange("(k p) n -> p k n", p=P)).then_inc(s_wrel, 16)
                sp.wait_ge(s_wrel, 16 * (r + 1))
            with sp.Fori(0, REL) as r:
                for t in range(NT):
                    sp.wait_ge(s_evac, r * NT + (NT + t + 1))
                    sp.dma_start(msg_t[ds(r * NT + t, 1), :, :].rearrange("a p d -> (a p) d"),
                                 stage[:, t % 5, :]).then_inc(s_tab[t % 5], 16)
            sp.wait_ge(s_prod, NT * (REL + 1))
            sp.dma_start(w1_v, w1.rearrange("(k p) n -> p k n", p=P)).then_inc(s_ffw, 16)
            sp.dma_start(w2_v, w2.rearrange("(k p) n -> p k n", p=P)).then_inc(s_ffw, 16)

            sp.wait_ge(c_f, NT)
            sp.wait_ge(d_tab, 1)

            def load_w(t, u):
                e = sp.value_load(texp[0:1, ds(t, 1)], min_val=0, max_val=EXPERTS - 1)
                sp.dma_start(ew_v[:, u, :], flat_rows(experts[ds(e, 1), :, :])).then_inc(e_w[u], 16)

            def load_x(t, u):
                sp.dma_start(xs[:, u, :], flat_rows(xslot_t[ds(t, 1), :, :])).then_inc(e_x[u], 16)

            def store(t, u):
                sp.wait_ge(e_yt, t + 1)
                sp.dma_start(flat_rows(yslot_t[ds(t, 1), :, :]), ys[:, u, :]).then_inc(e_out[u], 16)

            for u in range(MR):
                load_w(u, u)
            sp.wait_ge(d_sc, 16 * 2 * NT)
            for u in range(MR):
                load_x(u, u)
            with sp.Fori(0, SLOT_TILES // MR - 1) as it:
                for u in range(MR):
                    store(it * MR + u, u)
                    load_w(it * MR + (u + MR), u)
                    load_x(it * MR + (u + MR), u)
            for u in range(MR):
                store(SLOT_TILES - MR + u, u)
            for t in range(NT):
                sp.wait_ge(f_done, t + 1)
                sp.dma_start(out.rearrange("(t p) d -> t p d", p=P)[t], x_res[:, t, :]).then_inc(f_out, 16)
            sp.wait_ge(f_out, 16 * NT)

        @block.gpsimd
        def _(pool):
            own = Steps(s_pool)
            nc.gpsimd.iota(num[:, :], pattern=[[1, PAIRS]], base=0, channel_multiplier=0,
                           allow_small_or_imprecise_dtypes=True).then_inc(s_cst, 1)
            nc.gpsimd.memset(mhalf[:, :], -0.5).then_inc(s_cst, 1)
            own.did(nc.gpsimd.memset(ident[:, :], 0.0))
            own.did(nc.gpsimd.memset(tri_incl[:, :], 0.0))
            own.did(nc.gpsimd.memset(tri_bf[:, :], 0.0))
            nc.gpsimd.memset(ones[:, :], 1.0).then_inc(s_cst, 1)
            nc.gpsimd.memset(ones_bf[:, :], 1.0).then_inc(s_cst, 1)
            pool.wait_ge(s_pool, own.now())
            nc.gpsimd.affine_select(out=ident[:, :], in_=ident[:, :], compare_op=ALU.not_equal, fill=1.0,
                                    base=0, pattern=[[-1, P]], channel_multiplier=1).then_inc(s_cst, 1)
            nc.gpsimd.affine_select(out=tri_incl[:, :], in_=tri_incl[:, :], compare_op=ALU.is_gt, fill=1.0,
                                    base=0, pattern=[[-1, P]], channel_multiplier=1).then_inc(s_cst, 1)
            nc.gpsimd.affine_select(out=tri_bf[:, :], in_=tri_bf[:, :], compare_op=ALU.is_ge, fill=1.0,
                                    base=0, pattern=[[-1, P]], channel_multiplier=1).then_inc(s_cst, 1)
            for u in range(GROUP):
                n = NT * AW // GROUP
                nc.gpsimd.memset(agg[:, u * n:(u + 1) * n], 0.0).then_inc(s_sums, 1)
            pool.wait_ge(s_cst, 2)
            pool.wait_ge(s_var, 1)
            nc.gpsimd.tensor_tensor(rs[:, :], var[:, :], mhalf[:, :], ALU.pow).then_inc(s_rs, 1)
            pool.wait_ge(s_off, 1)
            for h, n in ((0, P), (1, EC - P)):
                own.did(nc.gpsimd.tensor_scalar(le_end[h][0:n, :], num[0:n, :], s_end[0:n, h:h + 1], None, ALU.is_ge))
                own.did(nc.gpsimd.tensor_scalar(le_beg[h][0:n, :], num[0:n, :], s_beg[0:n, h:h + 1], None, ALU.is_ge))
            pool.wait_ge(s_pool, own.now())
            for h, n in ((0, P), (1, EC - P)):
                own.did(nc.gpsimd.tensor_tensor(le_beg[h][0:n, :], le_beg[h][0:n, :], le_end[h][0:n, :], ALU.subtract))
                own.did(nc.gpsimd.tensor_scalar(in_blk[h][0:n, :], num[0:n, :], a_off[0:n, h:h + 1], None, ALU.add))
            pool.wait_ge(s_pool, own.now())
            for h, n in ((0, P), (1, EC - P)):
                nc.gpsimd.tensor_tensor(in_blk[h][0:n, :], in_blk[h][0:n, :], le_beg[h][0:n, :],
                                        ALU.mult).then_inc(s_mask, 1)
            pool.wait_ge(s_vec, 16)
            for t in range(NT):
                pool.wait_ge(s_xnT, t + 1)
                nc.gpsimd.tensor_tensor(work[:, t, :], work[:, t, :], vec[:, V_SELF, :], ALU.add).then_inc(s_sb, 1)

            for u in range(5):
                pool.wait_ge(s_tab[u], 16 * REL * NT // 5)
            pool.wait_ge(s_idx, 1)
            pool.wait_ge(s_tabc, 8)

            next_group = Turn(pool, s_idx, 2, 1)

            def gathers(it0, it1):
                with pool.Fori(it0, it1) as it:
                    for g in range(3):
                        for u in range(g * GROUP, (g + 1) * GROUP):
                            nc.gpsimd.indirect_dma_start(
                                gath[:, u, :], None, msg,
                                bass.IndirectOffsetOnAxis(ap=row_i[:, u:u + 1], axis=0)).then_inc(s_gath[u], 16)
                        next_group.wait()

            gathers(0, FAST)
            n = pool.value_load(npair[0:1, 0:1], min_val=1, max_val=EC * NT)
            with pool.If(n > FAST * RING):
                gathers(FAST, ALL)

            cp = Steps(c_pool)

            def power(s):
                pool.wait_ge(c_var, cp.now() + 1)
                cp.n += 1
                nc.gpsimd.tensor_tensor(sm[:, s, 3:4], sm[:, s, 2:3], mhalf[:, 0:1], ALU.pow).then_inc(c_rs, 1)

            x1_there = Turn(pool, c_x1, 1, 1)

            def first_norm(it):
                for s in range(2):
                    power(s)
                for s in range(2):
                    x1_there.wait()
                    t = it * 2 + s
                    nc.gpsimd.tensor_tensor(flat(work[:, ds(t, 1), :]), x1[:, s, :], vec[:, V_F2, :],
                                            ALU.add).then_inc(c_x1b, 1)

            def other_norms():
                for _ in range(2):
                    for s in range(2):
                        power(s)

            first_norm(0)
            first_norm(1)
            with pool.Fori(0, NT // 2 - 2) as it:
                cp.loop(it, 6)
                other_norms()
                first_norm(it + 2)
            cp.end(NT // 2 - 2)
            other_norms()
            other_norms()

            pool.wait_ge(d_pos, 1)
            pool.wait_ge(s_zero, 16)
            for t in range(NT):
                for c in range(2):
                    nc.gpsimd.indirect_dma_start(
                        xslot, bass.IndirectOffsetOnAxis(ap=pos_i[:, 2 * t + c:2 * t + c + 1], axis=0),
                        work[:, t, :], None).then_inc(d_sc, 16)
            for u in range(MR):
                pool.wait_ge(e_out[u], 16 * SLOT_TILES // MR)
            for t in range(NT):
                if t >= 4:
                    pool.wait_ge(f_done, t - 3)
                for c in range(2):
                    nc.gpsimd.indirect_dma_start(
                        yg[:, t % 4, c, :], None, yslot,
                        bass.IndirectOffsetOnAxis(ap=pos_i[:, 2 * t + c:2 * t + c + 1], axis=0)).then_inc(f_g[t % 4], 16)

        @block.scalar
        def _(act):
            act.dma_start(vec[:, :, :], vecs.rearrange("v d -> (v d)").partition_broadcast(P)
                          .rearrange("p (v d) -> p v d", v=NV)).then_inc(s_vec, 16)
            act.dma_start(bf1_s[:, :], bf1).then_inc(s_ffw, 16)
            act.dma_start(rw_s[:, :, :], rwT.rearrange("(k p) e -> p k e", p=P)).then_inc(s_ffw, 16)
            act.dma_start(rb_s[:, :], rb.partition_broadcast(P)).then_inc(s_ffw, 16)
            act.dma_start(eb2_s[:, :], eb2).then_inc(s_ffw, 16)
            for t in range(NT):
                act.wait_ge(s_xnT, t + 1)
                nc.scalar.copy(xT[:, t, :, :].rearrange("p k n -> p (k n)"), bank(5 + t % 3)).then_inc(s_xTc, 1)
            act.wait_ge(s_sums, GROUP)
            act.dma_start(xslot.rearrange("(t p) d -> p t d", p=P),
                          agg[:, 0:D].unsqueeze(1).to_broadcast([P, SLOT_TILES, D])).then_inc(s_zero, 16)
            for q in range(8):
                act.wait_ge(s_tabp, q + 1)
                tab, p0 = (ctab, 0) if q < 4 else (btab, 32)
                nc.scalar.copy(tab[:, (q % 4) * PIECE:(q % 4 + 1) * PIECE],
                               ps[p0:p0 + 1, (5 + q % 2) * D:(5 + q % 2) * D + PIECE])\
                    .then_inc(s_tabc, 1)
            act.wait_ge(s_tabc, 8)
            act.wait_ge(s_etab, 3)

            def lay_out(c, u):
                nc.scalar.copy(dw[:, u, :], dstw[:, ds(c, 1), :].rearrange("p a b -> p (a b)"))
                return nc.scalar.copy(row_i[:, u:u + 1], erow[:, ds(c, 1)])

            def chunks_from(i):
                return several(nc, mybir.EngineType.Activation, ctab[:, ds(i, RING)], EC)

            cs = chunks_from(0)
            for g in range(3):
                for u in range(GROUP):
                    last = lay_out(cs[g * GROUP + u], g * GROUP + u)
                last.then_inc(s_idx, 1)

            group_added = Turn(act, s_sums, 2 * GROUP, GROUP)

            def indices(it0, it1):
                with act.Fori(it0, it1) as it:
                    cs = chunks_from((it + 1) * RING)
                    for g in range(3):
                        group_added.wait()
                        for u in range(GROUP):
                            last = lay_out(cs[g * GROUP + u], g * GROUP + u)
                        last.then_inc(s_idx, 1)

            indices(0, FAST)
            n = act.value_load(npair[0:1, 0:1], min_val=1, max_val=EC * NT)
            with act.If(n > FAST * RING):
                indices(FAST, ALL)

            act.wait_ge(s_ffw, 16 * 6)
            act.wait_ge(s_aggd, 1)

            def copy_x1T(it):
                for s in range(2):
                    act.wait_ge(c_x1T, it * 2 + (s + 1))
                    nc.scalar.copy(x1T[:, :, s, :], bank(s).rearrange("p (k n) -> p k n", k=KD)).then_inc(c_x1Tc, 1)

            def hidden(it):
                if not isinstance(it, int) or it > 0:
                    act.wait_ge(c_f, it * 2)
                for f in range(KF):
                    act.wait_ge(c_h, it * KF + (f + 1))
                    nc.scalar.activation(hT[:, f, :], bank(4 + f % 4, 0, 2 * P), ACT.Gelu,
                                         bias=bf1_s[:, f:f + 1]).then_inc(c_g, 1)

            def copy_xmT(it):
                for s in range(2):
                    act.wait_ge(c_xmT, it * 2 + (s + 1))
                    nc.scalar.copy(xmT[:, s, :, :].rearrange("p k n -> p (k n)"), bank(4 + s)).then_inc(c_xmTc, 1)

            logits_there = Turn(act, c_lg, 1, 1)

            def copy_logits(it):
                for s in range(2):
                    logits_there.wait()
                    nc.scalar.copy(flat(lg[:, ds(it * 2 + s, 1), :]), bank(6 + s, 0, EXPERTS)).then_inc(c_lgt, 1)

            copy_x1T(0)
            hidden(0)
            copy_x1T(1)
            with act.Fori(0, NT // 2 - 2) as it:
                hidden(it + 1)
                copy_xmT(it)
                copy_x1T(it + 2)
                copy_logits(it)
            hidden(NT // 2 - 1)
            for it in (NT // 2 - 2, NT // 2 - 1):
                copy_xmT(it)
                copy_logits(it)

            act.wait_ge(d_lg0, 1)
            nc.scalar.activation(lg[:, :, :], lg[:, :, :], ACT.Exp).then_inc(d_ex, 1)
            for t in range(NT):
                act.wait_ge(d_gT, t + 1)
                nc.scalar.copy(gT[:, t, :], ps[0:EXPERTS, (2 + t % 2) * D:(2 + t % 2) * D + P]).then_inc(d_gTc, 1)

            def expert(t, u):
                m = SCR[u]
                act.wait_ge(e_xT, t + 1)
                nc.scalar.copy(xsT[:, m, :, :].rearrange("p k n -> p (k n)"), bank(m)).then_inc(e_xTc, 1)
                act.wait_ge(e_h, t + 1)
                for f in range(KE):
                    nc.scalar.activation(ehT[:, m, f, :], bank(6 + u % 2, f * P, P), ACT.Gelu,
                                         bias=ew_v[:, u, EW - KE + f:EW - KE + f + 1]).then_inc(e_g, 1)

            with act.Fori(0, SLOT_TILES // MR) as it:
                for u in range(MR):
                    expert(it * MR + u, u)

        @block.tensor
        def _(pe):
            pe.wait_ge(s_cst, 7)
            pe.wait_ge(s_blk, 1)
            nc.tensor.transpose(bank(7, 0, P), blk_f[:, 0:P], ident[:, :])
            nc.tensor.transpose(ps[0:EC - P, 7 * D + P:7 * D + 2 * P], blk_f[:, P:EC], ident[:, :]).then_inc(s_blkT, 1)
            pe.wait_ge(s_npc, 2)
            rest = EC - P
            nc.tensor.matmul(bank(7, 256, 1), tri_incl[:, :], npc[:, 0:1], start=True, stop=True)
            nc.tensor.matmul(ps[0:rest, 7 * D + 257:7 * D + 258], ones[:, 0:rest], npc[:, 0:1], start=True, stop=False)
            nc.tensor.matmul(ps[0:rest, 7 * D + 257:7 * D + 258], tri_incl[0:rest, 0:rest], npc[0:rest, 1:2],
                             start=False, stop=True)
            nc.tensor.matmul(bank(7, 258, 1), ones[:, :], npc[:, 0:1], start=True, stop=False)
            nc.tensor.matmul(bank(7, 258, 1), ones[0:rest, :], npc[0:rest, 1:2], start=False, stop=True)\
                .then_inc(s_pre, 1)
            for t in range(NT):
                pe.wait_ge(s_xn, t + 1)
                if t == 2:
                    pe.wait_ge(s_off, 1)
                if t >= 3:
                    pe.wait_ge(s_xTc, t - 2)
                for k in range(KD):
                    tr = nc.tensor.transpose(bank(5 + t % 3, k * P, P), work[:, t, k * P:(k + 1) * P], ident[:, :])
                tr.then_inc(s_xnT, 1)
            pe.wait_ge(s_wself, 16)
            for t in range(NT):
                pe.wait_ge(s_xTc, t + 1)
                if t >= 5:
                    pe.wait_ge(s_evac, t - 4)
                for k in range(KD):
                    mm = nc.tensor.matmul(bank(t % 5), xT[:, t, k, :], ws_v[:, k, :], start=(k == 0), stop=(k == KD - 1))
                mm.then_inc(s_prod, 1)
            pe.wait_ge(s_mask, 2)
            for q in range(8):
                if q >= 2:
                    pe.wait_ge(s_tabc, q - 1)
                m = le_end if q < 4 else in_blk
                p0 = 0 if q < 4 else 32
                o = ps[p0:p0 + 1, (5 + q % 2) * D:(5 + q % 2) * D + PIECE]
                c = slice((q % 4) * PIECE, (q % 4 + 1) * PIECE)
                nc.tensor.matmul(o, ones_bf[:, 0:1], m[0][:, c], start=True, stop=False)
                nc.tensor.matmul(o, ones_bf[0:rest, 0:1], m[1][0:rest, c], start=False, stop=True).then_inc(s_tabp, 1)
            with pe.Fori(0, REL) as r:
                pe.wait_ge(s_wrel, r * 16 + 16)
                for t in range(NT):
                    pe.wait_ge(s_evac, r * NT + (NT + t - 4))
                    for k in range(KD):
                        mm = nc.tensor.matmul(bank(t % 5), xT[:, t, k, :], wr_v[:, ds(r * (KD * D) + k * D, D)],
                                              start=(k == 0), stop=(k == KD - 1))
                    mm.then_inc(s_prod, 1)

            pe.wait_ge(s_evac, NT * (REL + 1))
            pe.wait_ge(s_tabc, 8)

            def sums(it0, it1):
                with pe.Fori(it0, it1) as it:
                    for u in range(RING):
                        pe.wait_ge(s_gath[u], it * 16 + 16)
                        pe.wait_ge(s_sel, it * RING + (u + 1))
                        pe.wait_ge(s_sums, it * RING + (u + 1))
                        b = 2 * (u % GROUP)
                        nc.tensor.matmul(bank(b), sel[:, u, :], gath[:, u, :], start=True, stop=True)
                        nc.tensor.matmul(bank(b + 1, 0, 1), sel[:, u, :], ones[:, 0:1], start=True, stop=True)\
                            .then_inc(s_mm, 1)

            sums(0, FAST)
            n = pe.value_load(npair[0:1, 0:1], min_val=1, max_val=EC * NT)
            with pe.If(n > FAST * RING):
                sums(FAST, ALL)

            pe.wait_ge(s_aggd, 1)
            pe.wait_ge(s_ffw, 16 * 6)

            def turn_x1(it):
                for s in range(2):
                    pe.wait_ge(c_x1, it * 2 + (s + 1))
                    for k in range(KD):
                        tr = nc.tensor.transpose(bank(s, k * P, P), x1[:, s, k * P:(k + 1) * P], ident[:, :])
                    tr.then_inc(c_x1T, 1)

            def ffn(it, first=False):
                for f in range(KF):
                    if f == 0:
                        pe.wait_ge(c_x1Tc, it * 2 + 2)
                    if not first or f >= 4:
                        pe.wait_ge(c_g, it * KF + (f - 3))
                    for k in range(KD):
                        mm = nc.tensor.matmul(bank(4 + f % 4, 0, 2 * P), w1_v[:, k, f * P:(f + 1) * P],
                                              x1T[:, k, :, :].rearrange("p s n -> p (s n)"),
                                              start=(k == 0), stop=(k == KD - 1))
                    mm.then_inc(c_h, 1)
                for s in range(2):
                    if not first:
                        pe.wait_ge(c_ft, it * 2 + (s - 1))
                    for f in range(KF):
                        if s == 0:
                            pe.wait_ge(c_g, it * KF + (f + 1))
                        mm = nc.tensor.matmul(bank(2 + s), hT[:, f, s * P:(s + 1) * P], w2_v[:, f, :],
                                              start=(f == 0), stop=(f == KF - 1))
                    mm.then_inc(c_f, 1)

            def turn_xm(it):
                for s in range(2):
                    pe.wait_ge(c_xm, it * 2 + (s + 1))
                    for k in range(KD):
                        tr = nc.tensor.transpose(bank(4 + s, k * P, P), xm[:, s, k * P:(k + 1) * P], ident[:, :])
                    tr.then_inc(c_xmT, 1)

            def logits(it):
                for s in range(2):
                    pe.wait_ge(c_xmTc, it * 2 + (s + 1))
                    for k in range(KD):
                        mm = nc.tensor.matmul(bank(6 + s, 0, EXPERTS), xmT[:, s, k, :], rw_s[:, k, :],
                                              start=(k == 0), stop=(k == KD - 1))
                    mm.then_inc(c_lg, 1)
                pe.wait_ge(c_lgt, it * 2 + 2)

            turn_x1(0)
            ffn(0, first=True)
            turn_x1(1)
            with pe.Fori(0, NT // 2 - 2) as it:
                ffn(it + 1)
                turn_xm(it)
                turn_x1(it + 2)
                logits(it)
            ffn(NT // 2 - 1)
            for it in (NT // 2 - 2, NT // 2 - 1):
                turn_xm(it)
                logits(it)

            pe.wait_ge(d_oh, 1)
            nc.tensor.matmul(bank(0, 0, R), tri_bf[:, :], oh_bf, start=True, stop=True)
            nc.tensor.matmul(bank(1, 0, R), ones_bf[:, :], oh_bf, start=True, stop=True).then_inc(d_cnt, 1)
            pe.wait_ge(d_gall, 1)
            for t in range(NT):
                if t >= 2:
                    pe.wait_ge(d_gTc, t - 1)
                nc.tensor.transpose(ps[0:EXPERTS, (2 + t % 2) * D:(2 + t % 2) * D + P], gate_all[:, t, :],
                                    ident[:, :]).then_inc(d_gT, 1)
            for t in range(NT):
                pe.wait_ge(d_gTc, t + 1)
                if t >= 4:
                    pe.wait_ge(d_b2t, t - 3)
                nc.tensor.matmul(bank(4 + t % 4), gT[:, t, :], eb2_s[:, :], start=True, stop=True).then_inc(d_b2, 1)
            pe.wait_ge(d_b2t, NT)

            def ahead(sem_, val):
                if not isinstance(val, int) or val > 0:
                    pe.wait_ge(sem_, val)

            def first_product(t, u, nth):
                m = SCR[u]
                pe.wait_ge(e_x[u], nth)
                ahead(e_xTc, t - 1)
                for k in range(KD):
                    tr = nc.tensor.transpose(bank(m, k * P, P), xs[:, u, k * P:(k + 1) * P], ident[:, :])
                tr.then_inc(e_xT, 1)
                pe.wait_ge(e_w[u], nth)
                pe.wait_ge(e_xTc, t + 1)
                ahead(e_g, t * KE)
                for f in range(KE):
                    for k in range(KD):
                        mm = nc.tensor.matmul(bank(6 + u % 2, f * P, P),
                                              ew_v[:, u, k * EF + f * P:k * EF + (f + 1) * P], xsT[:, m, k, :],
                                              start=(k == 0), stop=(k == KD - 1))
                mm.then_inc(e_h, 1)

            def second_product(t, u):
                m = SCR[u]
                pe.wait_ge(e_g, t * KE + KE)
                ahead(e_yt, t - 1)
                for f in range(KE):
                    mm = nc.tensor.matmul(bank(3 + m), ehT[:, m, f, :],
                                          ew_v[:, u, KD * EF + f * D:KD * EF + (f + 1) * D],
                                          start=(f == 0), stop=(f == KE - 1))
                mm.then_inc(e_y, 1)

            def expert_tiles(it, last=False):
                for u in range(MR):
                    if u < MR - 1:
                        first_product(it * MR + (u + 1), u + 1, it * 16 + 16)
                    elif not last:
                        first_product(it * MR + (u + 1), 0, it * 16 + 32)
                    second_product(it * MR + u, u)

            first_product(0, 0, 16)
            expert_tiles(0)
            with pe.Fori(1, SLOT_TILES // MR - 1) as it:
                expert_tiles(it)
            expert_tiles(SLOT_TILES // MR - 1, last=True)

        @block.vector
        def _(dve):
            v = nc.vector
            own = Steps(s_dve)

            def sync(steps):
                dve.wait_ge(steps.sem, steps.now())

            dve.wait_ge(s_edge, 64)
            own.did(v.tensor_scalar(blk_i[:, :], dst_i[:, :], BLOCK_SHIFT, None, ALU.logical_shift_right))
            own.did(v.tensor_scalar(erow[:, :], typ_i[:, :], float(NP), None, ALU.mult))
            sync(own)
            v.tensor_copy(blk_f[:, :], blk_i[:, :]).then_inc(s_blk, 1)
            v.tensor_copy(dstw[:, :, 0], dst_i[:, :]).then_inc(s_etab, 1)
            v.tensor_copy(dstw[:, :, 1], w_e[:, :]).then_inc(s_etab, 1)
            v.tensor_tensor(erow[:, :], erow[:, :], src_i[:, :], ALU.add).then_inc(s_etab, 1)
            dve.wait_ge(s_blkT, 1)
            for h, n in ((0, P), (1, EC - P)):
                blkT = ps[0:n, 7 * D + h * P:7 * D + (h + 1) * P]
                own.did(v.tensor_reduce(lohi[0:n, h, 0:1], blkT, AX.X, ALU.min))
                own.did(v.tensor_reduce(lohi[0:n, h, 1:2], blkT, AX.X, ALU.max))
            sync(own)
            for h, n in ((0, P), (1, EC - P)):
                v.scalar_tensor_tensor(out=npc[0:n, h:h + 1], in0=lohi[0:n, h, 1:2], scalar=1.0,
                                       in1=lohi[0:n, h, 0:1], op0=ALU.add, op1=ALU.subtract).then_inc(s_npc, 1)
            dve.wait_ge(s_x, 16)
            for t in range(NT):
                own.did(v.bn_stats(st[:, t, :], x_res[:, t, :]))
            sync(own)
            for t in range(NT):
                own.did(v.bn_aggr(mv[:, t, :], st[:, t, :]))
            sync(own)
            v.tensor_scalar(var[:, :], mv[:, :, 1], EPS, None, ALU.add).then_inc(s_var, 1)
            dve.wait_ge(s_pre, 1)
            dve.wait_ge(s_npc, 2)
            for h, n in ((0, P), (1, EC - P)):
                own.did(v.tensor_copy(s_end[0:n, h:h + 1], ps[0:n, 7 * D + 256 + h:7 * D + 257 + h]))
            own.did(v.tensor_copy(npair[0:1, 0:1], ps[0:1, 7 * D + 258:7 * D + 259]))
            sync(own)
            for h, n in ((0, P), (1, EC - P)):
                own.did(v.tensor_tensor(s_beg[0:n, h:h + 1], s_end[0:n, h:h + 1], npc[0:n, h:h + 1], ALU.subtract))
            sync(own)
            for h, n in ((0, P), (1, EC - P)):
                own.did(v.tensor_tensor(a_off[0:n, h:h + 1], lohi[0:n, h, 0:1], s_beg[0:n, h:h + 1], ALU.subtract))
            sync(own)
            v.tensor_copy(mv[:, 0, 1:2], var[:, 0:1]).then_inc(s_off, 1)
            dve.wait_ge(s_rs, 1)
            for t in range(NT):
                v.tensor_scalar(work[:, t, :], x_res[:, t, :], mv[:, t, 0:1], rs[:, t:t + 1],
                                ALU.subtract, ALU.mult).then_inc(s_xn, 1)
            dve.wait_ge(s_vec, 16)
            for t in range(NT):
                dve.wait_ge(s_sb, t + 1)
                dve.wait_ge(s_prod, t + 1)
                v.tensor_tensor(work[:, t, :], work[:, t, :], bank(t % 5), ALU.add).then_inc(s_evac, 1)
            with dve.Fori(0, REL) as r:
                for t in range(NT):
                    dve.wait_ge(s_prod, r * NT + (NT + t + 1))
                    if t >= 5:
                        dve.wait_ge(s_tab[t - 5], r * 32 + 16)
                    v.tensor_tensor(stage[:, t % 5, :], bank(t % 5), flat(vec[:, ds(r + V_REL, 1), :]),
                                    ALU.add).then_inc(s_evac, 1)
                for u in range(5):
                    dve.wait_ge(s_tab[u], r * 32 + 32)

            dve.wait_ge(s_tabc, 8)
            dve.wait_ge(s_zero, 16)
            dve.wait_ge(s_cst, 1)

            def tiles_of(first, n):
                return several(nc, mybir.EngineType.DVE, btab[:, ds(first, n)], NT - 1)

            def one_hot(bs, g, nth):
                dve.wait_ge(s_idx, nth)
                for u in range(GROUP):
                    i = g * GROUP + u
                    v.tensor_scalar(sel[:, i, :], num[:, ds(bs[u] * P, P)], dw[:, i, 0:1], dw[:, i, 1:2],
                                    ALU.is_equal, ALU.mult).then_inc(s_sel, 1)

            def add(bs, it, g):
                for u in range(GROUP):
                    i = g * GROUP + u
                    dve.wait_ge(s_mm, it * RING + (i + 1))
                    dve.wait_ge(s_sums, it * RING + (i + GROUP))
                    sums = agg[:, ds(bs[u] * AW, D + 1)]
                    v.tensor_tensor(sums, sums, ps[:, 2 * u * D:2 * u * D + D + 1], ALU.add).then_inc(s_sums, 1)

            one_hot(tiles_of(0, GROUP), 0, 1)

            def aggregate(it0, it1):
                with dve.Fori(it0, it1) as it:
                    tiles = tiles_of(it * RING, RING + GROUP)
                    for g in range(3):
                        one_hot(tiles[(g + 1) * GROUP:(g + 2) * GROUP], (g + 1) % 3, it * 3 + (g + 2))
                        add(tiles[g * GROUP:(g + 1) * GROUP], it, g)

            aggregate(0, FAST)
            n = dve.value_load(npair[0:1, 0:1], min_val=1, max_val=EC * NT)
            with dve.If(n > FAST * RING):
                aggregate(FAST, ALL)
            v.tensor_copy(sm[:, 0, 0:1], ones[:, 0:1]).then_inc(s_aggd, 1)
            dve.wait_ge(s_aggd, 1)

            cs = Steps(c_dve)
            rsn = Steps(c_rs)

            def stats(t, s):
                cs.did(v.bn_stats(st[:, s, :], t))

            def norm_stats(srcs):
                for s in range(2):
                    cs.did(v.bn_stats(st[:, s, :], srcs[s]))
                sync(cs)
                cs.did(v.memset(sm[:, 0, 4:5], 0.0))
                for s in range(2):
                    cs.did(v.bn_aggr(mv[:, s, :], st[:, s, :]))
                sync(cs)
                for s in range(2):
                    v.tensor_scalar(sm[:, s, 2:3], mv[:, s, 1:2], EPS, None, ALU.add).then_inc(c_var, 1)

            def scaled(srcs, gain):
                for s in range(2):
                    cs.did(v.scalar_tensor_tensor(out=tmp[:, s, :], in0=srcs[s], scalar=mv[:, s, 0:1],
                                                  in1=vec[:, gain, :], op0=ALU.subtract, op1=ALU.mult))
                sync(cs)
                rsn.n += 2
                sync(rsn)

            def first_norm(it):
                for s in range(2):
                    t = it * 2 + s
                    cs.did(v.tensor_scalar(sm[:, s, 0:1], agg[:, ds(t * AW + D, 1)], 1.0, None, ALU.max))
                sync(cs)
                for s in range(2):
                    cs.did(v.reciprocal(sm[:, s, 1:2], sm[:, s, 0:1]))
                sync(cs)
                for s in range(2):
                    t = it * 2 + s
                    cs.did(v.scalar_tensor_tensor(out=h1[:, s, :], in0=agg[:, ds(t * AW, D)], scalar=sm[:, s, 1:2],
                                                  in1=flat(work[:, ds(t, 1), :]), op0=ALU.mult, op1=ALU.add))
                sync(cs)
                norm_stats([h1[:, s, :] for s in range(2)])
                scaled([h1[:, s, :] for s in range(2)], V_G1)
                for s in range(2):
                    if not isinstance(it, int) or it > 0:
                        dve.wait_ge(c_x1T, it * 2 + (s - 1))
                        dve.wait_ge(c_x1b, it * 2 + (s - 1))
                    v.scalar_tensor_tensor(out=x1[:, s, :], in0=tmp[:, s, :], scalar=sm[:, s, 3:4],
                                           in1=vec[:, V_B1, :], op0=ALU.mult, op1=ALU.add).then_inc(c_x1, 1)
                dve.wait_ge(c_x1, it * 2 + 2)

            def other_norms(it):
                for s in range(2):
                    dve.wait_ge(c_f, it * 2 + (s + 1))
                    dve.wait_ge(c_x1b, it * 2 + (s + 1))
                    v.tensor_tensor(y1[:, s, :], flat(work[:, ds(it * 2 + s, 1), :]), bank(2 + s),
                                    ALU.add).then_inc(c_ft, 1)
                dve.wait_ge(c_ft, it * 2 + 2)
                ys_ = [y1[:, s, :] for s in range(2)]
                norm_stats(ys_)
                scaled(ys_, V_G2)
                for s in range(2):
                    cs.did(v.scalar_tensor_tensor(out=y1[:, s, :], in0=tmp[:, s, :], scalar=sm[:, s, 3:4],
                                                  in1=vec[:, V_B2, :], op0=ALU.mult, op1=ALU.add))
                sync(cs)
                for s in range(2):
                    cs.did(v.tensor_tensor(y1[:, s, :], y1[:, s, :], flat(x_res[:, ds(it * 2 + s, 1), :]), ALU.add))
                sync(cs)
                norm_stats(ys_)
                for s in range(2):
                    cs.did(v.tensor_scalar(flat(x_res[:, ds(it * 2 + s, 1), :]), y1[:, s, :], 1.0, None, ALU.mult))
                rsn.n += 2
                sync(rsn)
                for s in range(2):
                    v.tensor_scalar(xm[:, s, :], y1[:, s, :], mv[:, s, 0:1], sm[:, s, 3:4],
                                    ALU.subtract, ALU.mult).then_inc(c_xm, 1)
                for s in range(2):
                    cs.did(v.tensor_scalar(flat(work[:, ds(it * 2 + s, 1), :]), y1[:, s, :], mv[:, s, 0:1],
                                           sm[:, s, 3:4], ALU.subtract, ALU.mult))
                sync(cs)

            first_norm(0)
            first_norm(1)
            with dve.Fori(0, NT // 2 - 2) as it:
                cs.loop(it, 33)
                rsn.loop(it, 6)
                other_norms(it)
                first_norm(it + 2)
                dve.wait_ge(c_xmT, it * 2 + 2)
            cs.end(NT // 2 - 2)
            rsn.end(NT // 2 - 2)
            other_norms(NT // 2 - 2)
            dve.wait_ge(c_xmT, NT - 2)
            other_norms(NT // 2 - 1)

            rd = Steps(d_dve)

            def did(ins):
                rd.did(ins)
                sync(rd)

            per_t = [P, NT, EXPERTS]
            dve.wait_ge(c_lgt, NT)
            did(v.tensor_tensor(lg[:, :, :], lg[:, :, :], rb_s[:, :].unsqueeze(1).to_broadcast(per_t), ALU.add))
            did(v.tensor_reduce(var[:, :], lg[:, :, :], AX.X, ALU.max))
            v.tensor_tensor(lg[:, :, :], lg[:, :, :], var[:, :].unsqueeze(2).to_broadcast(per_t),
                            ALU.subtract).then_inc(d_lg0, 1)
            dve.wait_ge(d_ex, 1)
            did(v.tensor_reduce(var[:, :], lg[:, :, :], AX.X, ALU.add))
            did(v.reciprocal(rs[:, :], var[:, :]))
            did(v.tensor_tensor(probs, lg[:, :, :], rs[:, :].unsqueeze(2).to_broadcast(per_t), ALU.mult))
            for t in range(NT):
                rd.did(v.max(m8[:, t, :], probs[:, t, :]))
            sync(rd)
            for t in range(NT):
                rd.did(v.max_index(i8[:, t, :], m8[:, t, :], probs[:, t, :]))
            sync(rd)
            did(v.tensor_copy(idx_f[:, :, :], i8[:, :, 0:2]))
            for c, e in ((0, e1), (1, e2)):
                rd.did(v.tensor_tensor(e, num[:, 0:EXPERTS].unsqueeze(1).to_broadcast(per_t),
                                       idx_f[:, :, c:c + 1].to_broadcast(per_t), ALU.is_equal))
            sync(rd)
            v.tensor_tensor(oh_bf, flat(e1), flat(e2), ALU.add).then_inc(d_oh, 1)
            rd.did(v.tensor_tensor(gate_all, e1, m8[:, :, 0:1].to_broadcast(per_t), ALU.mult))
            rd.did(v.tensor_tensor(prod, e2, m8[:, :, 1:2].to_broadcast(per_t), ALU.mult))
            rd.did(v.memset(cum[:, 0, :], 0.0))
            sync(rd)
            v.tensor_tensor(gate_all, gate_all, prod, ALU.add).then_inc(d_gall, 1)
            dve.wait_ge(d_cnt, 1)
            for t in range(NT):
                did(v.tensor_tensor(cum[:, t + 1, :], cum[:, t, :], bank(1, t * EXPERTS, EXPERTS), ALU.add))
            did(v.tensor_scalar(cnt_i[:, :], cum[:, NT, :], float(P - 1), None, ALU.add))
            did(v.tensor_scalar(cnt_i[:, :], cnt_i[:, :], BLOCK_SHIFT, None, ALU.logical_shift_right))
            did(v.tensor_copy(row16[:, 0, :], cnt_i[:, :]))
            did(v.tensor_tensor_scan(row16[:, 1, :], ones[:, 0:EXPERTS], row16[:, 0, :], 0.0, ALU.mult, ALU.add))
            tab = [1, SLOT_TILES + 1, EXPERTS]
            did(v.tensor_tensor(tcmp[:, :, :], num[0:1, 0:SLOT_TILES + 1].unsqueeze(2).to_broadcast(tab),
                                row16[0:1, 1:2, :].to_broadcast(tab), ALU.is_ge))
            did(v.tensor_reduce(texp_f[:, :], tcmp[:, :, :], AX.X, ALU.add))
            v.tensor_scalar(texp[:, :], texp_f[:, :], float(EXPERTS - 1), None, ALU.min).then_inc(d_tab, 1)
            did(v.tensor_tensor(row16[:, 2, :], row16[:, 1, :], row16[:, 0, :], ALU.subtract))
            rd.did(v.tensor_scalar(row16[:, 3, :], row16[:, 2, :], float(P), None, ALU.mult))
            did(v.tensor_tensor(rank, cum[:, 0:NT, :], bank(0, 0, R).rearrange("p (t e) -> p t e", e=EXPERTS), ALU.add))
            did(v.tensor_tensor(rank, rank, row16[:, 3:4, :].to_broadcast(per_t), ALU.add))
            for c, e in ((0, e1), (1, e2)):
                did(v.tensor_tensor(prod, e, rank, ALU.mult))
                did(v.tensor_reduce(pos_f[:, :, c], prod, AX.X, ALU.add))
            v.tensor_copy(pos_i[:, :], flat(pos_f[:, :, :])).then_inc(d_pos, 1)
            for t in range(NT):
                dve.wait_ge(d_b2, t + 1)
                v.tensor_tensor(x_res[:, t, :], x_res[:, t, :], bank(4 + t % 4), ALU.add).then_inc(d_b2t, 1)

            def take(t, u):
                dve.wait_ge(e_y, t + 1)
                v.tensor_copy(ys[:, u, :], bank(3 + SCR[u])).then_inc(e_yt, 1)

            for u in range(MR):
                take(u, u)
            with dve.Fori(1, SLOT_TILES // MR) as it:
                for u in range(MR):
                    dve.wait_ge(e_out[u], it * 16)
                    take(it * MR + u, u)

            dve.wait_ge(d_b2t, NT)
            for t in range(NT):
                dve.wait_ge(f_g[t % 4], 32 * (t // 4 + 1))
                v.scalar_tensor_tensor(out=x_res[:, t, :], in0=yg[:, t % 4, 0, :], scalar=m8[:, t, 0:1],
                                       in1=x_res[:, t, :], op0=ALU.mult, op1=ALU.add).then_inc(f_dve, 1)
                dve.wait_ge(f_dve, t + 1)
                v.scalar_tensor_tensor(out=x_res[:, t, :], in0=yg[:, t % 4, 1, :], scalar=m8[:, t, 1:2],
                                       in1=x_res[:, t, :], op0=ALU.mult, op1=ALU.add).then_inc(f_done, 1)


def kernel(**inputs):
    import numpy as np
    import concourse.bacc as bacc
    from concourse.bass_utils import run_bass_kernel_spmd

    a = {k: np.ascontiguousarray(v) for k, v in inputs.items()}

    def chunks(v, fill):
        full = np.full((ECP * P,), fill, v.dtype)
        full[0:EDGES] = v
        return np.ascontiguousarray(full.reshape(ECP, P).T)

    x = np.zeros((NP, D), a["x"].dtype)
    x[0:NODES] = a["x"]
    experts = np.concatenate([
        a["L0_ffn_w1"].reshape(EXPERTS, EF, KD, P).transpose(0, 3, 2, 1).reshape(EXPERTS, P, KD * EF),
        a["L0_ffn_w2"].reshape(EXPERTS, D, KE, P).transpose(0, 3, 2, 1).reshape(EXPERTS, P, KE * D),
        a["L0_ffn_b1"].reshape(EXPERTS, KE, P).transpose(0, 2, 1)], axis=2)
    vecs = np.concatenate([a["L0_gnn_b_self"][None], a["L0_gnn_b_rel"]]
                          + [a["L0_gnn_" + n][None] for n in ("ln1_g", "ln1_b", "ln2_g", "ln2_b", "b_ffn2")], axis=0)
    arrays = {
        "x": x, "src": chunks(a["src"], 0), "dst": chunks(a["dst"], NODES - 1), "typ": chunks(a["edge_type_4"], 0),
        "wgt": chunks(a["edge_weight"], 0), "w_self": a["L0_gnn_W_self"], "w_rel": a["L0_gnn_W_rel"], "vecs": vecs,
        "w1": a["L0_gnn_W_ffn1"], "w2": a["L0_gnn_W_ffn2"],
        "bf1": np.ascontiguousarray(a["L0_gnn_b_ffn1"].reshape(KF, P).T),
        "rwT": np.ascontiguousarray(a["L0_ffn_router_w"].T), "rb": a["L0_ffn_router_b"],
        "experts": np.ascontiguousarray(experts), "eb2": a["L0_ffn_b2"],
    }
    nc = bacc.Bacc("TRN2", target_bir_lowering=False, num_devices=1)
    args = [nc.dram_tensor(n, v.shape, mybir.dt.from_np(v.dtype), kind="ExternalInput").ap() for n, v in arrays.items()]
    out = nc.dram_tensor("out", (NP, D), F32, kind="ExternalOutput").ap()
    program(nc, *args, out)
    r = run_bass_kernel_spmd(nc, [arrays], core_ids=[0])
    return r.results[0]["out"][0:NODES]
```

```python
from contextlib import ExitStack

import concourse.bass as bass
from concourse import mybir

F32 = mybir.dt.float32
F32R = mybir.dt.float32r
BF16 = mybir.dt.bfloat16
I32 = mybir.dt.int32
U32 = mybir.dt.uint32
ALU = mybir.AluOpType
ACT = mybir.ActivationFunctionType
AX = mybir.AxisListType
ds = bass.ds

P = 128
D = 512
KD = D // P
NODES = 1250
NT = -(-NODES // P)
NP = NT * P
EDGES = 20000
EC = -(-EDGES // P)
ECP = EC + 1
REL = 4
FF = 1024
KF = FF // P
EPS = 1e-5

GROUP = 4
RING = 3 * GROUP
FAST = -(-(EC + NT - 1) // RING)
ALL = -(-EC * NT // RING)
PAIRS = (ALL + 1) * RING
PIECE = PAIRS // 4
AW = D + 2
BLOCK_SHIFT = 7

EXPERTS = 16
EF = 256
KE = EF // P
SLOT_TILES = (2 * NP + EXPERTS * (P - 1)) // P
EW = KD * EF + KE * D + KE
MR = 5
USUAL = -(-2 * NP // P) + EXPERTS // 2
LOOPED = USUAL // MR
FREE = 5
assert SLOT_TILES % MR == 0 and PAIRS % 4 == 0 and NT % 2 == 0

V_SELF, V_REL, V_G1, V_B1, V_G2, V_B2, V_F2, NV = 0, 1, 5, 6, 7, 8, 9, 10


def several(nc, engine, table, most):
    _, values = nc.values_load_multi_w_load_instructions(
        table, engines=(engine,), min_val=0, max_val=most,
        skip_runtime_bounds_check_because="the table is worked out from sums that stay within the bounds")
    return values


class Turn:

    def __init__(self, eng, sem, first, step):
        self.eng, self.sem, self.step = eng, sem, step
        self.reg = eng.alloc_register()
        eng.reg_mov(self.reg, first)

    def wait(self):
        self.eng.wait_ge(self.sem, self.reg)
        self.eng.reg_add(self.reg, self.reg, self.step)


class Steps:

    def __init__(self, sem):
        self.sem, self.n, self.at, self.per = sem, 0, None, 0

    def loop(self, it, per):
        self.at, self.per, self.first = it, per, self.n

    def end(self, trips):
        assert self.n - self.first == self.per, (self.n - self.first, self.per)
        self.n = self.first + self.per * trips
        self.at = None

    def did(self, ins):
        ins.then_inc(self.sem, 1)
        self.n += 1

    def now(self):
        return self.n if self.at is None else self.at * self.per + self.n


def program(nc, x, src, dst, typ, wgt, w_self, w_rel, vecs, w1, w2, bf1, rwT, rb, experts, eb2, out):
    ctx = ExitStack()
    with ctx:
        def sb(name, shape, dt=F32):
            return ctx.enter_context(nc.sbuf_tensor(name, shape, dt))

        def sem(name):
            return ctx.enter_context(nc.semaphore(name))

        msg = nc.dram_tensor("msg", (REL * NP, D), F32, kind="Internal").ap()
        xslot = nc.dram_tensor("xslot", (SLOT_TILES * P, D), F32, kind="Internal").ap()
        yslot = nc.dram_tensor("yslot", (SLOT_TILES * P, D), F32, kind="Internal").ap()

        def early(*tensors):
            with ExitStack() as early_ctx:
                return [early_ctx.enter_context(nc.sbuf_tensor(*a)) for a in tensors]

        ident = sb("ident", [P, P])
        ones = sb("ones", [P, P])
        tri_incl = sb("tri_incl", [P, P])
        ones_bf = sb("ones_bf", [P, P], BF16)
        tri_bf = sb("tri_bf", [P, P], BF16)
        num = sb("num", [P, PAIRS])
        vec = sb("vec", [P, NV, D])
        w_hi, w_lo, w_in = early(("w_hi", [P, 2, KD * D], F32R), ("w_lo", [P, 2, KD * D], F32R),
                                 ("w_in", [P, KD * D], F32))
        wreg = sb("wreg", [P, MR * EW])
        xT_lo, = early(("xT_lo", [P, NT * D], F32R))
        x_res = sb("x_res", [P, NT, D])
        work = sb("work", [P, NT, D])
        agg = sb("agg", [P, NT * AW])
        greg = sb("greg", [P, RING * D])
        xT_hi, = early(("xT_hi", [P, NT * D], F32R))
        treg = sb("treg", [P, NT * D + 5 * D])
        sel = sb("sel", [P, RING, P])
        src_i, dst_i, typ_i, blk_i = (sb(n, [P, ECP], I32) for n in ("src_i", "dst_i", "typ_i", "blk_i"))
        w_e = sb("w_e", [P, ECP])
        erow = sb("erow", [P, ECP])
        blk_f = sb("blk_f", [P, ECP])
        dstw = sb("dstw", [P, ECP, 2])
        dw = sb("dw", [P, RING, 2])
        row_i = sb("row_i", [P, RING], I32)
        lohi = sb("lohi", [P, 2, 2])
        npc = sb("npc", [P, 2])
        s_end = sb("s_end", [P, 2])
        s_beg = sb("s_beg", [P, 2])
        a_off = sb("a_off", [P, 2])
        npair = sb("npair", [1, 2], I32)
        steps = sb("steps", [33, PAIRS], I32)
        ctab = steps[0:1, :]
        btab = steps[32:33, :]
        st = sb("st", [P, NT, 6])
        mv = sb("mv", [P, NT, 2])
        var = sb("var", [P, NT])
        rs = sb("rs", [P, NT])
        mhalf = sb("mhalf", [P, NT])
        sm = sb("sm", [P, 2, 8])
        bf1_s = sb("bf1_s", [P, KF])
        rw_s = sb("rw_s", [P, KD, EXPERTS])
        rb_s = sb("rb_s", [P, EXPERTS])
        lg = sb("lg", [P, NT, EXPERTS])
        eb2_s = sb("eb2_s", [EXPERTS, D])
        ps = ctx.enter_context(nc.psum_tensor("ps", [P, 8 * D], F32))

        def flat(ap):
            return ap.rearrange("p a b -> p (a b)")

        def flat_rows(ap):
            return ap.rearrange("a p n -> (a p) n")

        def bank(i, a=0, n=D):
            return ps[:, i * D + a:i * D + a + n]

        w1_v = wreg[:, 0:KD * FF].rearrange("p (k n) -> p k n", k=KD)
        w2_v = wreg[:, KD * FF:KD * FF + KF * D].rearrange("p (k n) -> p k n", k=KF)
        ew_v = wreg[:, 0:MR * EW].rearrange("p (u n) -> p u n", u=MR)
        stage = treg[:, NT * D:].rearrange("p (u n) -> p u n", u=5)
        gath = greg[:, :].rearrange("p (u n) -> p u n", u=RING)
        HB = PAIRS // 2

        def bfrow(i):
            return greg[:, i * HB:(i + 1) * HB].bitcast(BF16)

        le_end = [bfrow(0), bfrow(1)]
        in_blk = [bfrow(2), bfrow(3)]
        le_beg = [bfrow(4), bfrow(5)]
        h1 = greg[:, 0:2 * D].rearrange("p (s n) -> p s n", s=2)
        x1 = greg[:, 2 * D:4 * D].rearrange("p (s n) -> p s n", s=2)
        hT = greg[:, 6 * D:10 * D].rearrange("p (k n) -> p k n", k=KF)
        tmp = greg[:, 10 * D:12 * D].rearrange("p (s n) -> p s n", s=2)
        x1T = treg[:, 0:2 * D].rearrange("p (k s n) -> p k s n", k=KD, s=2)
        xm = treg[:, 2 * D:4 * D].rearrange("p (s n) -> p s n", s=2)
        xmT = treg[:, 4 * D:6 * D].rearrange("p (s k n) -> p s k n", s=2, k=KD)
        y1 = treg[:, 6 * D:8 * D].rearrange("p (s n) -> p s n", s=2)
        zeros = sel[:, 0:D // P, :].rearrange("p k n -> p (k n)")
        R = NT * EXPERTS
        xs = greg[:, 0:MR * D].rearrange("p (u n) -> p u n", u=MR)
        ys = greg[:, MR * D:2 * MR * D].rearrange("p (u n) -> p u n", u=MR)
        SCR = (0, 1, 2, 0, 1)
        xsT = treg[:, 0:3 * D].rearrange("p (s k n) -> p s k n", s=3, k=KD)
        ehT = treg[:, 3 * D:3 * D + 3 * EF].rearrange("p (s k n) -> p s k n", s=3, k=KE)
        yg = greg[:, 0:8 * D].rearrange("p (u c n) -> p u c n", u=4, c=2)

        rt = treg[:, 12 * D:15 * D]

        def rslot(i, n=R):
            return rt[:, i * R:i * R + n].rearrange("p (t e) -> p t e", e=EXPERTS) if n == R else rt[:, i * R:i * R + n]

        e1 = rslot(0)
        e2 = rslot(1)
        rank = rslot(2)
        prod = rslot(3)
        probs = rslot(4)
        oh_bf = rt[:, 5 * R:5 * R + R // 2].bitcast(BF16)
        gate_all = rslot(6)
        cum = rt[:, 7 * R:7 * R + R + EXPERTS].rearrange("p (t e) -> p t e", e=EXPERTS)
        m8 = sb("m8", [P, NT, 8])
        i8 = sb("i8", [P, NT, 8], U32)
        idx_f = sb("idx_f", [P, NT, 2])
        pos_f = sb("pos_f", [P, NT, 2])
        pos_i = sb("pos_i", [P, NT * 2], I32)
        row16 = sb("row16", [P, 8, EXPERTS])
        cnt_i = sb("cnt_i", [P, EXPERTS], I32)
        tcmp = treg[0:1, 8 * D:8 * D + (SLOT_TILES + 1) * EXPERTS].rearrange("p (t e) -> p t e", e=EXPERTS)
        texp_f = sb("texp_f", [1, SLOT_TILES + 1])
        texp = sb("texp", [1, SLOT_TILES + 1], I32)
        gT = agg[0:EXPERTS, 0:NT * P].rearrange("p (t n) -> p t n", t=NT)

        s_dst = sem("destinations_in")
        s_xh = [sem(f"x_half_in{h}") for h in range(2)]
        s_x = sem("x_in_again")
        s_edge = sem("edges_in")
        s_vec = sem("vecs_in")
        s_win = sem("product_weights_in")
        s_whi = sem("product_weights_high_part")
        s_wlo = sem("product_weights_low_part")
        s_cst = sem("constants")
        s_dve = sem("dve_step")
        s_blk = sem("edge_tiles")
        s_blkT = sem("edge_tiles_transposed")
        s_npc = sem("pairs_per_chunk")
        s_pre = sem("pair_prefix")
        s_off = sem("pair_offsets")
        s_pool = sem("pool_step")
        s_mask = sem("step_masks")
        s_tabp = sem("table_piece")
        s_tabc = sem("table_copied")
        s_var = sem("variances")
        s_rs = sem("one_over_sigma")
        s_xn = sem("x_normed")
        s_xnT = sem("x_transposed")
        s_xhi = sem("x_transposed_high_part")
        s_xlo = sem("x_transposed_low_part")
        s_sb = sem("b_self_added")
        s_prod = sem("product_ready")
        s_evac = sem("product_taken")
        s_tab = [sem(f"msg_rows_out{u}") for u in range(5)]
        s_zeros = sem("zeros_ready")
        s_zero = sem("xslot_cleared")
        s_etab = sem("edge_table")
        s_idx = sem("step_indices")
        s_gath = [sem(f"gathered{u}") for u in range(RING)]
        s_sel = sem("one_hot_ready")
        s_mm = sem("step_product")
        s_sums = sem("sums_written")
        s_aggd = sem("aggregated")
        s_ffw = sem("ffn_weights_in")
        c_dve = sem("node_dve_step")
        c_var = sem("node_variance")
        c_rs = sem("node_one_over_sigma")
        c_pool = sem("node_pool_step")
        c_x1 = sem("x1_ready")
        c_x1T = sem("x1_transposed")
        c_x1Tc = sem("x1_transposed_in_sbuf")
        c_x1b = sem("x1_plus_bias")
        c_h = sem("hidden_product")
        c_g = sem("hidden_gelu")
        c_f = sem("ffn_product")
        c_ft = sem("ffn_taken")
        c_xm = sem("expert_input_ready")
        c_xmT = sem("expert_input_transposed")
        c_xmTc = sem("expert_input_T_in_sbuf")
        c_lg = sem("logits_product")
        c_lgt = sem("logits_taken")
        d_dve = sem("route_dve_step")
        d_lg0 = sem("logits_centred")
        d_ex = sem("logits_exp")
        d_oh = sem("one_hots")
        d_cnt = sem("counts_product")
        d_tab = sem("expert_table")
        d_pos = sem("slots_ready")
        d_sc = sem("rows_scattered")
        d_gall = sem("gates_ready")
        d_gT = sem("gates_transposed")
        d_gTc = sem("gates_T_in_sbuf")
        d_b2 = sem("bias_product")
        d_b2t = sem("bias_taken")
        e_w = [sem(f"expert_weights_in{u}") for u in range(MR)]
        e_x = [sem(f"slot_rows_in{u}") for u in range(MR)]
        e_xT = sem("slot_rows_transposed")
        e_xTc = sem("slot_rows_T_in_sbuf")
        e_h = sem("expert_hidden_product")
        e_g = sem("expert_hidden_gelu")
        e_y = sem("expert_product")
        e_yt = sem("expert_product_taken")
        e_out = [sem(f"slot_rows_out{u}") for u in range(MR)]
        f_g = [sem(f"results_gathered{u}") for u in range(4)]
        f_dve = sem("combine_step")
        f_done = sem("tile_combined")
        f_out = sem("out_written")

        def load_product_weights(eng, i):
            w = w_rel[i] if i < REL else w_self
            eng.dma_start(w_in[:, :].rearrange("p (k n) -> p k n", k=KD),
                          w.rearrange("(k p) n -> p k n", p=P)).then_inc(s_win, 16)

        def tiles_used(eng):
            return eng.value_load(npair[0:1, 1:2], min_val=1, max_val=SLOT_TILES)

        FFN_LOADS = 4 + KD + KF // 2
        msg_t = msg.rearrange("(r t p) d -> (r t) p d", r=REL, p=P)
        xslot_t = xslot.rearrange("(t p) d -> t p d", p=P)
        yslot_t = yslot.rearrange("(t p) d -> t p d", p=P)

        block = ctx.enter_context(nc.Block())

        @block.sync
        def _(sp):
            sp.dma_start(dst_i[:, :], dst).then_inc(s_dst, 16)
            for h in range(2):
                a, b = h * NT // 2, (h + 1) * NT // 2
                sp.dma_start(x_res[:, a:b, :], x[a * P:b * P, :].rearrange("(t p) d -> p t d", p=P)).then_inc(s_xh[h], 16)
            load_product_weights(sp, 0)
            for a, b in ((src_i, src), (typ_i, typ), (w_e, wgt)):
                sp.dma_start(a[:, :], b).then_inc(s_edge, 16)
            with sp.Fori(0, REL) as r:
                for t in range(NT):
                    sp.wait_ge(s_evac, r * NT + (FREE + t + 1))
                    sp.dma_start(msg_t[ds(r * NT + t, 1), :, :].rearrange("a p d -> (a p) d"),
                                 stage[:, t % 5, :]).then_inc(s_tab[t % 5], 16)
            sp.wait_ge(s_prod, NT * (REL + 1))
            pieces = [(w1_v[:, k, :], w1[k * P:(k + 1) * P, :], s_ffw) for k in range(KD)]
            pieces += [(w2_v[:, k:k + 2, :], w2[k * P:(k + 2) * P, :].rearrange("(k p) n -> p k n", p=P), s_ffw)
                       for k in range(0, KF, 2)]
            pieces += [(x_res[:, t:t + 2, :], x[t * P:(t + 2) * P, :].rearrange("(t p) d -> p t d", p=P), s_x)
                       for t in range(0, NT, 2)]
            for i, (to, of, landed) in enumerate(pieces):
                sp.wait_ge(s_sums, GROUP + min(i + 1, FAST) * RING)
                sp.dma_start(to, of).then_inc(landed, 16)
            sp.wait_ge(s_zeros, 1)
            for rows in (xslot, yslot[USUAL * P:, :]):
                n = rows.shape[0] // P
                sp.dma_start(rows.rearrange("(t p) d -> p t d", p=P),
                             zeros.unsqueeze(1).to_broadcast([P, n, D])).then_inc(s_zero, 16)

            sp.wait_ge(c_f, NT)
            sp.wait_ge(d_tab, 1)

            def load_w(t, u):
                e = sp.value_load(texp[0:1, ds(t, 1)], min_val=0, max_val=EXPERTS - 1)
                sp.dma_start(ew_v[:, u, :], flat_rows(experts[ds(e, 1), :, :])).then_inc(e_w[u], 16)

            def load_x(t, u):
                sp.dma_start(xs[:, u, :], flat_rows(xslot_t[ds(t, 1), :, :])).then_inc(e_x[u], 16)

            def store(t, u):
                sp.wait_ge(e_yt, t + 1)
                sp.dma_start(flat_rows(yslot_t[ds(t, 1), :, :]), ys[:, u, :]).then_inc(e_out[u], 16)

            for u in range(2):
                load_w(u, u)
            sp.wait_ge(d_sc, 16 * 2 * NT)
            for u in range(2):
                load_x(u, u)
            for u in range(2, MR):
                load_w(u, u)
                load_x(u, u)
            with sp.Fori(0, LOOPED - 1) as it:
                for u in range(MR):
                    store(it * MR + u, u)
                    load_w(it * MR + (u + MR), u)
                    load_x(it * MR + (u + MR), u)

            def rest(first, end):
                for t in range(first, end):
                    store(t, t % MR)
                    if t + MR < end:
                        load_w(t + MR, t % MR)
                        load_x(t + MR, t % MR)

            rest((LOOPED - 1) * MR, USUAL)
            with sp.If(tiles_used(sp) > USUAL):
                for t in range(USUAL, min(USUAL + MR, SLOT_TILES)):
                    load_w(t, t % MR)
                    load_x(t, t % MR)
                rest(USUAL, SLOT_TILES)
            for t in range(NT):
                sp.wait_ge(f_done, t + 1)
                sp.dma_start(out.rearrange("(t p) d -> t p d", p=P)[t], x_res[:, t, :]).then_inc(f_out, 16)
            sp.wait_ge(f_out, 16 * NT)

        @block.gpsimd
        def _(pool):
            own = Steps(s_pool)
            nc.gpsimd.iota(num[:, :], pattern=[[1, PAIRS]], base=0, channel_multiplier=0,
                           allow_small_or_imprecise_dtypes=True).then_inc(s_cst, 1)
            nc.gpsimd.memset(mhalf[:, :], -0.5).then_inc(s_cst, 1)
            nc.gpsimd.memset(sm[:, 0, 7:8], 0.0).then_inc(s_evac, FREE)
            own.did(nc.gpsimd.memset(ident[:, :], 0.0))
            own.did(nc.gpsimd.memset(tri_incl[:, :], 0.0))
            own.did(nc.gpsimd.memset(tri_bf[:, :], 0.0))
            nc.gpsimd.memset(ones[:, :], 1.0).then_inc(s_cst, 1)
            nc.gpsimd.memset(ones_bf[:, :], 1.0).then_inc(s_cst, 1)
            pool.wait_ge(s_pool, own.now())
            nc.gpsimd.affine_select(out=ident[:, :], in_=ident[:, :], compare_op=ALU.not_equal, fill=1.0,
                                    base=0, pattern=[[-1, P]], channel_multiplier=1).then_inc(s_cst, 1)
            nc.gpsimd.affine_select(out=tri_incl[:, :], in_=tri_incl[:, :], compare_op=ALU.is_gt, fill=1.0,
                                    base=0, pattern=[[-1, P]], channel_multiplier=1).then_inc(s_cst, 1)
            nc.gpsimd.affine_select(out=tri_bf[:, :], in_=tri_bf[:, :], compare_op=ALU.is_ge, fill=1.0,
                                    base=0, pattern=[[-1, P]], channel_multiplier=1).then_inc(s_cst, 1)
            for u in range(GROUP):
                n = NT * AW // GROUP
                nc.gpsimd.memset(agg[:, u * n:(u + 1) * n], 0.0).then_inc(s_sums, 1)
            pool.wait_ge(s_cst, 2)
            for h in range(2):
                half = slice(h * NT // 2, (h + 1) * NT // 2)
                pool.wait_ge(s_var, h + 1)
                nc.gpsimd.tensor_tensor(rs[:, half], var[:, half], mhalf[:, half], ALU.pow).then_inc(s_rs, 1)
            pool.wait_ge(s_whi, 1)
            nc.gpsimd.tensor_tensor(w_lo[:, 0, :], w_in[:, :], w_hi[:, 0, :], ALU.subtract).then_inc(s_wlo, 1)
            pool.wait_ge(s_off, 2)
            for h, n in ((0, P), (1, EC - P)):
                own.did(nc.gpsimd.tensor_scalar(le_end[h][0:n, :], num[0:n, :], s_end[0:n, h:h + 1], None, ALU.is_ge))
                own.did(nc.gpsimd.tensor_scalar(le_beg[h][0:n, :], num[0:n, :], s_beg[0:n, h:h + 1], None, ALU.is_ge))
            pool.wait_ge(s_pool, own.now())
            for h, n in ((0, P), (1, EC - P)):
                own.did(nc.gpsimd.tensor_tensor(le_beg[h][0:n, :], le_beg[h][0:n, :], le_end[h][0:n, :], ALU.subtract))
                own.did(nc.gpsimd.tensor_scalar(in_blk[h][0:n, :], num[0:n, :], a_off[0:n, h:h + 1], None, ALU.add))
            pool.wait_ge(s_pool, own.now())
            for h, n in ((0, P), (1, EC - P)):
                nc.gpsimd.tensor_tensor(in_blk[h][0:n, :], in_blk[h][0:n, :], le_beg[h][0:n, :],
                                        ALU.mult).then_inc(s_mask, 1)
            pool.wait_ge(s_vec, 16)
            for t in range(NT):
                pool.wait_ge(s_xnT, t + 1)
                nc.gpsimd.tensor_tensor(work[:, t, :], work[:, t, :], vec[:, V_SELF, :], ALU.add).then_inc(s_sb, 1)

            for u in range(5):
                pool.wait_ge(s_tab[u], 16 * REL * NT // 5)
            pool.wait_ge(s_idx, 1)
            pool.wait_ge(s_tabc, 8)

            next_group = Turn(pool, s_idx, 2, 1)

            def gathers(it0, it1):
                with pool.Fori(it0, it1) as it:
                    for g in range(3):
                        for u in range(g * GROUP, (g + 1) * GROUP):
                            nc.gpsimd.indirect_dma_start(
                                gath[:, u, :], None, msg,
                                bass.IndirectOffsetOnAxis(ap=row_i[:, u:u + 1], axis=0)).then_inc(s_gath[u], 16)
                        next_group.wait()

            gathers(0, FAST)
            n = pool.value_load(npair[0:1, 0:1], min_val=1, max_val=EC * NT)
            with pool.If(n > FAST * RING):
                gathers(FAST, ALL)

            pool.wait_ge(s_aggd, 1)
            nc.gpsimd.memset(zeros, 0.0).then_inc(s_zeros, 1)

            cp = Steps(c_pool)

            def power(s):
                pool.wait_ge(c_var, cp.now() + 1)
                cp.n += 1
                nc.gpsimd.tensor_tensor(sm[:, s, 3:4], sm[:, s, 2:3], mhalf[:, 0:1], ALU.pow).then_inc(c_rs, 1)

            x1_there = Turn(pool, c_x1, 1, 1)

            def first_norm(it):
                for s in range(2):
                    power(s)
                for s in range(2):
                    x1_there.wait()
                    t = it * 2 + s
                    nc.gpsimd.tensor_tensor(flat(work[:, ds(t, 1), :]), x1[:, s, :], vec[:, V_F2, :],
                                            ALU.add).then_inc(c_x1b, 1)

            def other_norms():
                for _ in range(2):
                    for s in range(2):
                        power(s)

            first_norm(0)
            first_norm(1)
            with pool.Fori(0, NT // 2 - 2) as it:
                cp.loop(it, 6)
                other_norms()
                first_norm(it + 2)
            cp.end(NT // 2 - 2)
            other_norms()
            other_norms()

            pool.wait_ge(d_pos, 1)
            pool.wait_ge(s_zero, 32)
            for t in range(NT):
                for c in range(2):
                    nc.gpsimd.indirect_dma_start(
                        xslot, bass.IndirectOffsetOnAxis(ap=pos_i[:, 2 * t + c:2 * t + c + 1], axis=0),
                        work[:, t, :], None).then_inc(d_sc, 16)
            for t in range(USUAL - MR, USUAL):
                pool.wait_ge(e_out[t % MR], 16 * (t // MR + 1))
            with pool.If(tiles_used(pool) > USUAL):
                for t in range(SLOT_TILES - MR, SLOT_TILES):
                    pool.wait_ge(e_out[t % MR], 16 * (t // MR + 1))
            for t in range(NT):
                if t >= 4:
                    pool.wait_ge(f_done, t - 3)
                for c in range(2):
                    nc.gpsimd.indirect_dma_start(
                        yg[:, t % 4, c, :], None, yslot,
                        bass.IndirectOffsetOnAxis(ap=pos_i[:, 2 * t + c:2 * t + c + 1], axis=0)).then_inc(f_g[t % 4], 16)

        @block.scalar
        def _(act):
            act.wait_ge(s_win, 16)
            act.dma_start(vec[:, :, :], vecs.rearrange("v d -> (v d)").partition_broadcast(P)
                          .rearrange("p (v d) -> p v d", v=NV)).then_inc(s_vec, 16)
            act.dma_start(bf1_s[:, :], bf1).then_inc(s_ffw, 16)
            act.dma_start(rw_s[:, :, :], rwT.rearrange("(k p) e -> p k e", p=P)).then_inc(s_ffw, 16)
            act.dma_start(rb_s[:, :], rb.partition_broadcast(P)).then_inc(s_ffw, 16)
            act.dma_start(eb2_s[:, :], eb2).then_inc(s_ffw, 16)
            act.wait_ge(s_win, 16)
            nc.scalar.copy(w_hi[:, 0, :], w_in[:, :]).then_inc(s_whi, 1)
            for t in range(NT):
                act.wait_ge(s_xnT, t + 1)
                nc.scalar.copy(xT_hi[:, t * D:(t + 1) * D], bank(5 + t % 3)).then_inc(s_xhi, 1)
            for i in range(1, REL + 1):
                act.wait_ge(s_wlo, i)
                load_product_weights(act, i)
                act.wait_ge(s_win, 16 * (i + 1))
                if i >= 2:
                    act.wait_ge(s_prod, (i - 1) * NT)
                nc.scalar.copy(w_hi[:, i % 2, :], w_in[:, :]).then_inc(s_whi, 1)
            for q in range(8):
                act.wait_ge(s_tabp, q + 1)
                tab, p0 = (ctab, 0) if q < 4 else (btab, 32)
                nc.scalar.copy(tab[:, (q % 4) * PIECE:(q % 4 + 1) * PIECE],
                               ps[p0:p0 + 1, (5 + q % 2) * D:(5 + q % 2) * D + PIECE])\
                    .then_inc(s_tabc, 1)
            act.wait_ge(s_tabc, 8)
            act.wait_ge(s_etab, 3)

            def lay_out(c, u):
                nc.scalar.copy(dw[:, u, :], dstw[:, ds(c, 1), :].rearrange("p a b -> p (a b)"))
                return nc.scalar.copy(row_i[:, u:u + 1], erow[:, ds(c, 1)])

            def chunks_from(i):
                return several(nc, mybir.EngineType.Activation, ctab[:, ds(i, RING)], EC)

            cs = chunks_from(0)
            for g in range(3):
                for u in range(GROUP):
                    last = lay_out(cs[g * GROUP + u], g * GROUP + u)
                last.then_inc(s_idx, 1)

            group_added = Turn(act, s_sums, 2 * GROUP, GROUP)

            def indices(it0, it1):
                with act.Fori(it0, it1) as it:
                    cs = chunks_from((it + 1) * RING)
                    for g in range(3):
                        group_added.wait()
                        for u in range(GROUP):
                            last = lay_out(cs[g * GROUP + u], g * GROUP + u)
                        last.then_inc(s_idx, 1)

            indices(0, FAST)
            n = act.value_load(npair[0:1, 0:1], min_val=1, max_val=EC * NT)
            with act.If(n > FAST * RING):
                indices(FAST, ALL)

            act.wait_ge(s_ffw, FFN_LOADS * 16)
            act.wait_ge(s_aggd, 1)

            def copy_x1T(it):
                for s in range(2):
                    act.wait_ge(c_x1T, it * 2 + (s + 1))
                    nc.scalar.copy(x1T[:, :, s, :], bank(s).rearrange("p (k n) -> p k n", k=KD)).then_inc(c_x1Tc, 1)

            def hidden(it):
                if not isinstance(it, int) or it > 0:
                    act.wait_ge(c_f, it * 2)
                for f in range(KF):
                    act.wait_ge(c_h, it * KF + (f + 1))
                    nc.scalar.activation(hT[:, f, :], bank(4 + f % 4, 0, 2 * P), ACT.Gelu,
                                         bias=bf1_s[:, f:f + 1]).then_inc(c_g, 1)

            def copy_xmT(it):
                for s in range(2):
                    act.wait_ge(c_xmT, it * 2 + (s + 1))
                    nc.scalar.copy(xmT[:, s, :, :].rearrange("p k n -> p (k n)"), bank(4 + s)).then_inc(c_xmTc, 1)

            logits_there = Turn(act, c_lg, 1, 1)

            def copy_logits(it):
                for s in range(2):
                    logits_there.wait()
                    nc.scalar.copy(flat(lg[:, ds(it * 2 + s, 1), :]), bank(6 + s, 0, EXPERTS)).then_inc(c_lgt, 1)

            copy_x1T(0)
            hidden(0)
            copy_x1T(1)
            with act.Fori(0, NT // 2 - 2) as it:
                hidden(it + 1)
                copy_xmT(it)
                copy_x1T(it + 2)
                copy_logits(it)
            hidden(NT // 2 - 1)
            for it in (NT // 2 - 2, NT // 2 - 1):
                copy_xmT(it)
                copy_logits(it)

            act.wait_ge(d_lg0, 1)
            nc.scalar.activation(lg[:, :, :], lg[:, :, :], ACT.Exp).then_inc(d_ex, 1)
            for t in range(NT):
                act.wait_ge(d_gT, t + 1)
                nc.scalar.copy(gT[:, t, :], ps[0:EXPERTS, (2 + t % 2) * D:(2 + t % 2) * D + P]).then_inc(d_gTc, 1)

            def expert(t, u):
                m = SCR[u]
                act.wait_ge(e_xT, t + 1)
                nc.scalar.copy(xsT[:, m, :, :].rearrange("p k n -> p (k n)"), bank(m)).then_inc(e_xTc, 1)
                act.wait_ge(e_h, t + 1)
                for f in range(KE):
                    nc.scalar.activation(ehT[:, m, f, :], bank(6 + u % 2, f * P, P), ACT.Gelu,
                                         bias=ew_v[:, u, EW - KE + f:EW - KE + f + 1]).then_inc(e_g, 1)

            with act.Fori(0, LOOPED) as it:
                for u in range(MR):
                    expert(it * MR + u, u)
            for t in range(LOOPED * MR, USUAL):
                expert(t, t % MR)
            with act.If(tiles_used(act) > USUAL):
                for t in range(USUAL, SLOT_TILES):
                    expert(t, t % MR)

        @block.tensor
        def _(pe):
            pe.wait_ge(s_cst, 7)
            pe.wait_ge(s_blk, 1)
            nc.tensor.transpose(bank(4, 0, P), blk_f[:, 0:P], ident[:, :])
            nc.tensor.transpose(ps[0:EC - P, 4 * D + P:4 * D + 2 * P], blk_f[:, P:EC], ident[:, :]).then_inc(s_blkT, 1)
            for t in range(NT):
                pe.wait_ge(s_xn, t + 1)
                if t >= 3:
                    pe.wait_ge(s_xlo, t - 2)
                for k in range(KD):
                    tr = nc.tensor.transpose(bank(5 + t % 3, k * P, P), work[:, t, k * P:(k + 1) * P], ident[:, :])
                tr.then_inc(s_xnT, 1)
            pe.wait_ge(s_npc, 2)
            rest = EC - P
            nc.tensor.matmul(bank(4, 256, 1), tri_incl[:, :], npc[:, 0:1], start=True, stop=True)
            nc.tensor.matmul(ps[0:rest, 4 * D + 257:4 * D + 258], ones[:, 0:rest], npc[:, 0:1], start=True, stop=False)
            nc.tensor.matmul(ps[0:rest, 4 * D + 257:4 * D + 258], tri_incl[0:rest, 0:rest], npc[0:rest, 1:2],
                             start=False, stop=True)
            nc.tensor.matmul(bank(4, 258, 1), ones[:, :], npc[:, 0:1], start=True, stop=False)
            nc.tensor.matmul(bank(4, 258, 1), ones[0:rest, :], npc[0:rest, 1:2], start=False, stop=True)\
                .then_inc(s_pre, 1)
            def product(i, t, done):
                pe.wait_ge(s_evac, done + 1)
                for k in range(KD):
                    at = slice(t * D + k * P, t * D + (k + 1) * P)
                    wk = slice(k * D, (k + 1) * D)
                    nc.tensor.matmul(bank(t % 5), xT_hi[:, at], w_hi[:, i, wk], start=(k == 0), stop=False)
                    nc.tensor.matmul(bank(t % 5), xT_hi[:, at], w_lo[:, i, wk], start=False, stop=False)
                    mm = nc.tensor.matmul(bank(t % 5), xT_lo[:, at], w_hi[:, i, wk], start=False, stop=(k == KD - 1))
                mm.then_inc(s_prod, 1)

            pe.wait_ge(s_xlo, NT)
            with pe.Fori(0, REL // 2) as r2:
                for i in range(2):
                    pe.wait_ge(s_wlo, r2 * 2 + (i + 1))
                    for t in range(NT):
                        if t == 4:
                            pe.wait_ge(s_off, 2)
                        product(i, t, r2 * (2 * NT) + (i * NT + t))
            pe.wait_ge(s_mask, 2)
            for q in range(8):
                if q >= 2:
                    pe.wait_ge(s_tabc, q - 1)
                m = le_end if q < 4 else in_blk
                p0 = 0 if q < 4 else 32
                o = ps[p0:p0 + 1, (5 + q % 2) * D:(5 + q % 2) * D + PIECE]
                c = slice((q % 4) * PIECE, (q % 4 + 1) * PIECE)
                nc.tensor.matmul(o, ones_bf[:, 0:1], m[0][:, c], start=True, stop=False)
                nc.tensor.matmul(o, ones_bf[0:rest, 0:1], m[1][0:rest, c], start=False, stop=True).then_inc(s_tabp, 1)
            pe.wait_ge(s_wlo, REL + 1)
            for t in range(NT):
                product(REL % 2, t, REL * NT + t)

            pe.wait_ge(s_evac, NT * (REL + 1) + FREE)
            pe.wait_ge(s_tabc, 8)

            def sums(it0, it1):
                with pe.Fori(it0, it1) as it:
                    for u in range(RING):
                        pe.wait_ge(s_gath[u], it * 16 + 16)
                        pe.wait_ge(s_sel, it * RING + (u + 1))
                        pe.wait_ge(s_sums, it * RING + (u + 1))
                        b = 2 * (u % GROUP)
                        nc.tensor.matmul(bank(b), sel[:, u, :], gath[:, u, :], start=True, stop=True)
                        nc.tensor.matmul(bank(b + 1, 0, 1), sel[:, u, :], ones[:, 0:1], start=True, stop=True)\
                            .then_inc(s_mm, 1)

            sums(0, FAST)
            n = pe.value_load(npair[0:1, 0:1], min_val=1, max_val=EC * NT)
            with pe.If(n > FAST * RING):
                sums(FAST, ALL)

            pe.wait_ge(s_aggd, 1)
            pe.wait_ge(s_ffw, FFN_LOADS * 16)

            def turn_x1(it):
                for s in range(2):
                    pe.wait_ge(c_x1, it * 2 + (s + 1))
                    for k in range(KD):
                        tr = nc.tensor.transpose(bank(s, k * P, P), x1[:, s, k * P:(k + 1) * P], ident[:, :])
                    tr.then_inc(c_x1T, 1)

            def ffn(it, first=False):
                for f in range(KF):
                    if f == 0:
                        pe.wait_ge(c_x1Tc, it * 2 + 2)
                    if not first or f >= 4:
                        pe.wait_ge(c_g, it * KF + (f - 3))
                    for k in range(KD):
                        mm = nc.tensor.matmul(bank(4 + f % 4, 0, 2 * P), w1_v[:, k, f * P:(f + 1) * P],
                                              x1T[:, k, :, :].rearrange("p s n -> p (s n)"),
                                              start=(k == 0), stop=(k == KD - 1))
                    mm.then_inc(c_h, 1)
                for s in range(2):
                    if not first:
                        pe.wait_ge(c_ft, it * 2 + (s - 1))
                    for f in range(KF):
                        if s == 0:
                            pe.wait_ge(c_g, it * KF + (f + 1))
                        mm = nc.tensor.matmul(bank(2 + s), hT[:, f, s * P:(s + 1) * P], w2_v[:, f, :],
                                              start=(f == 0), stop=(f == KF - 1))
                    mm.then_inc(c_f, 1)

            def turn_xm(it):
                for s in range(2):
                    pe.wait_ge(c_xm, it * 2 + (s + 1))
                    for k in range(KD):
                        tr = nc.tensor.transpose(bank(4 + s, k * P, P), xm[:, s, k * P:(k + 1) * P], ident[:, :])
                    tr.then_inc(c_xmT, 1)

            def logits(it):
                for s in range(2):
                    pe.wait_ge(c_xmTc, it * 2 + (s + 1))
                    for k in range(KD):
                        mm = nc.tensor.matmul(bank(6 + s, 0, EXPERTS), xmT[:, s, k, :], rw_s[:, k, :],
                                              start=(k == 0), stop=(k == KD - 1))
                    mm.then_inc(c_lg, 1)
                pe.wait_ge(c_lgt, it * 2 + 2)

            turn_x1(0)
            ffn(0, first=True)
            turn_x1(1)
            with pe.Fori(0, NT // 2 - 2) as it:
                ffn(it + 1)
                turn_xm(it)
                turn_x1(it + 2)
                logits(it)
            ffn(NT // 2 - 1)
            for it in (NT // 2 - 2, NT // 2 - 1):
                turn_xm(it)
                logits(it)

            pe.wait_ge(d_oh, 1)
            nc.tensor.matmul(bank(0, 0, R), tri_bf[:, :], oh_bf, start=True, stop=True)
            nc.tensor.matmul(bank(1, 0, R), ones_bf[:, :], oh_bf, start=True, stop=True).then_inc(d_cnt, 1)
            pe.wait_ge(d_gall, 1)
            for t in range(NT):
                if t >= 2:
                    pe.wait_ge(d_gTc, t - 1)
                nc.tensor.transpose(ps[0:EXPERTS, (2 + t % 2) * D:(2 + t % 2) * D + P], gate_all[:, t, :],
                                    ident[:, :]).then_inc(d_gT, 1)
            for t in range(NT):
                pe.wait_ge(d_gTc, t + 1)
                if t >= 4:
                    pe.wait_ge(d_b2t, t - 3)
                nc.tensor.matmul(bank(4 + t % 4), gT[:, t, :], eb2_s[:, :], start=True, stop=True).then_inc(d_b2, 1)
            pe.wait_ge(d_b2t, NT)

            def ahead(sem_, val):
                if not isinstance(val, int) or val > 0:
                    pe.wait_ge(sem_, val)

            def first_product(t, u, nth):
                m = SCR[u]
                pe.wait_ge(e_x[u], nth)
                ahead(e_xTc, t - 1)
                for k in range(KD):
                    tr = nc.tensor.transpose(bank(m, k * P, P), xs[:, u, k * P:(k + 1) * P], ident[:, :])
                tr.then_inc(e_xT, 1)
                pe.wait_ge(e_w[u], nth)
                pe.wait_ge(e_xTc, t + 1)
                ahead(e_g, t * KE)
                for f in range(KE):
                    for k in range(KD):
                        mm = nc.tensor.matmul(bank(6 + u % 2, f * P, P),
                                              ew_v[:, u, k * EF + f * P:k * EF + (f + 1) * P], xsT[:, m, k, :],
                                              start=(k == 0), stop=(k == KD - 1))
                mm.then_inc(e_h, 1)

            def second_product(t, u):
                m = SCR[u]
                pe.wait_ge(e_g, t * KE + KE)
                ahead(e_yt, t - 1)
                for f in range(KE):
                    mm = nc.tensor.matmul(bank(3 + m), ehT[:, m, f, :],
                                          ew_v[:, u, KD * EF + f * D:KD * EF + (f + 1) * D],
                                          start=(f == 0), stop=(f == KE - 1))
                mm.then_inc(e_y, 1)

            def expert_tiles(it):
                for u in range(MR):
                    if u < MR - 1:
                        first_product(it * MR + (u + 1), u + 1, it * 16 + 16)
                    else:
                        first_product(it * MR + (u + 1), 0, it * 16 + 32)
                    second_product(it * MR + u, u)

            def rest_tiles(first, end):
                for t in range(first, end):
                    if t + 1 < end:
                        first_product(t + 1, (t + 1) % MR, (t + 1) // MR * 16 + 16)
                    second_product(t, t % MR)

            first_product(0, 0, 16)
            expert_tiles(0)
            with pe.Fori(1, LOOPED) as it:
                expert_tiles(it)
            rest_tiles(LOOPED * MR, USUAL)
            with pe.If(tiles_used(pe) > USUAL):
                first_product(USUAL, USUAL % MR, USUAL // MR * 16 + 16)
                rest_tiles(USUAL, SLOT_TILES)

        @block.vector
        def _(dve):
            v = nc.vector
            own = Steps(s_dve)

            def sync(steps):
                dve.wait_ge(steps.sem, steps.now())

            dve.wait_ge(s_dst, 16)
            own.did(v.tensor_scalar(blk_i[:, :], dst_i[:, :], BLOCK_SHIFT, None, ALU.logical_shift_right))
            sync(own)
            v.tensor_copy(blk_f[:, :], blk_i[:, :]).then_inc(s_blk, 1)
            for h in range(2):
                dve.wait_ge(s_xh[h], 16)
                tiles = range(h * NT // 2, (h + 1) * NT // 2)
                for t in tiles:
                    own.did(v.bn_stats(st[:, t, :], x_res[:, t, :]))
                sync(own)
                for t in tiles:
                    own.did(v.bn_aggr(mv[:, t, :], st[:, t, :]))
                sync(own)
                half = slice(tiles.start, tiles.stop)
                v.tensor_scalar(var[:, half], mv[:, half, 1], EPS, None, ALU.add).then_inc(s_var, 1)
            for t in range(NT):
                dve.wait_ge(s_rs, 1 if t < NT // 2 else 2)
                v.tensor_scalar(work[:, t, :], x_res[:, t, :], mv[:, t, 0:1], rs[:, t:t + 1],
                                ALU.subtract, ALU.mult).then_inc(s_xn, 1)
            dve.wait_ge(s_blkT, 1)
            for h, n in ((0, P), (1, EC - P)):
                blkT = ps[0:n, 4 * D + h * P:4 * D + (h + 1) * P]
                own.did(v.tensor_reduce(lohi[0:n, h, 0:1], blkT, AX.X, ALU.min))
                own.did(v.tensor_reduce(lohi[0:n, h, 1:2], blkT, AX.X, ALU.max))
            sync(own)
            for h, n in ((0, P), (1, EC - P)):
                v.scalar_tensor_tensor(out=npc[0:n, h:h + 1], in0=lohi[0:n, h, 1:2], scalar=1.0,
                                       in1=lohi[0:n, h, 0:1], op0=ALU.add, op1=ALU.subtract).then_inc(s_npc, 1)
            dve.wait_ge(s_xn, NT)
            for t in range(NT):
                dve.wait_ge(s_xhi, t + 1)
                part = slice(t * D, (t + 1) * D)
                v.tensor_tensor(xT_lo[:, part], bank(5 + t % 3), xT_hi[:, part], ALU.subtract).then_inc(s_xlo, 1)
            dve.wait_ge(s_pre, 1)
            dve.wait_ge(s_npc, 2)
            for h, n in ((0, P), (1, EC - P)):
                own.did(v.tensor_copy(s_end[0:n, h:h + 1], ps[0:n, 4 * D + 256 + h:4 * D + 257 + h]))
            own.did(v.tensor_copy(npair[0:1, 0:1], ps[0:1, 4 * D + 258:4 * D + 259]))
            sync(own)
            for h, n in ((0, P), (1, EC - P)):
                own.did(v.tensor_tensor(s_beg[0:n, h:h + 1], s_end[0:n, h:h + 1], npc[0:n, h:h + 1], ALU.subtract))
            sync(own)
            for h, n in ((0, P), (1, EC - P)):
                v.tensor_tensor(a_off[0:n, h:h + 1], lohi[0:n, h, 0:1], s_beg[0:n, h:h + 1],
                                ALU.subtract).then_inc(s_off, 1)
            dve.wait_ge(s_edge, 48)
            own.did(v.tensor_scalar(erow[:, :], typ_i[:, :], float(NP), None, ALU.mult))
            v.tensor_copy(dstw[:, :, 0], dst_i[:, :]).then_inc(s_etab, 1)
            v.tensor_copy(dstw[:, :, 1], w_e[:, :]).then_inc(s_etab, 1)
            sync(own)
            v.tensor_tensor(erow[:, :], erow[:, :], src_i[:, :], ALU.add).then_inc(s_etab, 1)

            def low_part(i, nth):
                dve.wait_ge(s_whi, nth)
                v.tensor_tensor(w_lo[:, i, :], w_in[:, :], w_hi[:, i, :], ALU.subtract).then_inc(s_wlo, 1)

            dve.wait_ge(s_vec, 16)
            with dve.Fori(0, REL // 2) as r2:
                for i in range(2):
                    low_part(1 - i, r2 * 2 + (i + 2))
                    for t in range(NT):
                        dve.wait_ge(s_prod, r2 * (2 * NT) + (i * NT + t + 1))
                        if t >= 5:
                            dve.wait_ge(s_tab[t - 5], r2 * 64 + (i * 32 + 16))
                        v.tensor_tensor(stage[:, t % 5, :], bank(t % 5), flat(vec[:, ds(r2 * 2 + (i + V_REL), 1), :]),
                                        ALU.add).then_inc(s_evac, 1)
                    for u in range(5):
                        dve.wait_ge(s_tab[u], r2 * 64 + (i * 32 + 32))
            for t in range(NT):
                dve.wait_ge(s_sb, t + 1)
                dve.wait_ge(s_prod, REL * NT + t + 1)
                v.tensor_tensor(work[:, t, :], work[:, t, :], bank(t % 5), ALU.add).then_inc(s_evac, 1)

            dve.wait_ge(s_tabc, 8)
            dve.wait_ge(s_sums, GROUP)
            dve.wait_ge(s_cst, 1)

            def tiles_of(first, n):
                return several(nc, mybir.EngineType.DVE, btab[:, ds(first, n)], NT - 1)

            def one_hot(bs, g, nth):
                dve.wait_ge(s_idx, nth)
                for u in range(GROUP):
                    i = g * GROUP + u
                    v.tensor_scalar(sel[:, i, :], num[:, ds(bs[u] * P, P)], dw[:, i, 0:1], dw[:, i, 1:2],
                                    ALU.is_equal, ALU.mult).then_inc(s_sel, 1)

            def add(bs, it, g):
                for u in range(GROUP):
                    i = g * GROUP + u
                    dve.wait_ge(s_mm, it * RING + (i + 1))
                    dve.wait_ge(s_sums, it * RING + (i + GROUP))
                    sums = agg[:, ds(bs[u] * AW, D + 1)]
                    v.tensor_tensor(sums, sums, ps[:, 2 * u * D:2 * u * D + D + 1], ALU.add).then_inc(s_sums, 1)

            one_hot(tiles_of(0, GROUP), 0, 1)

            def aggregate(it0, it1):
                with dve.Fori(it0, it1) as it:
                    tiles = tiles_of(it * RING, RING + GROUP)
                    for g in range(3):
                        one_hot(tiles[(g + 1) * GROUP:(g + 2) * GROUP], (g + 1) % 3, it * 3 + (g + 2))
                        add(tiles[g * GROUP:(g + 1) * GROUP], it, g)

            aggregate(0, FAST)
            n = dve.value_load(npair[0:1, 0:1], min_val=1, max_val=EC * NT)
            with dve.If(n > FAST * RING):
                aggregate(FAST, ALL)
            v.tensor_copy(sm[:, 0, 0:1], ones[:, 0:1]).then_inc(s_aggd, 1)
            dve.wait_ge(s_aggd, 1)

            dve.wait_ge(s_x, 16 * (NT // 2))
            cs = Steps(c_dve)
            rsn = Steps(c_rs)

            def stats(t, s):
                cs.did(v.bn_stats(st[:, s, :], t))

            def norm_stats(srcs):
                for s in range(2):
                    cs.did(v.bn_stats(st[:, s, :], srcs[s]))
                sync(cs)
                cs.did(v.memset(sm[:, 0, 4:5], 0.0))
                for s in range(2):
                    cs.did(v.bn_aggr(mv[:, s, :], st[:, s, :]))
                sync(cs)
                for s in range(2):
                    v.tensor_scalar(sm[:, s, 2:3], mv[:, s, 1:2], EPS, None, ALU.add).then_inc(c_var, 1)

            def scaled(srcs, gain):
                for s in range(2):
                    cs.did(v.scalar_tensor_tensor(out=tmp[:, s, :], in0=srcs[s], scalar=mv[:, s, 0:1],
                                                  in1=vec[:, gain, :], op0=ALU.subtract, op1=ALU.mult))
                sync(cs)
                rsn.n += 2
                sync(rsn)

            def first_norm(it):
                for s in range(2):
                    t = it * 2 + s
                    cs.did(v.tensor_scalar(sm[:, s, 0:1], agg[:, ds(t * AW + D, 1)], 1.0, None, ALU.max))
                sync(cs)
                for s in range(2):
                    cs.did(v.reciprocal(sm[:, s, 1:2], sm[:, s, 0:1]))
                sync(cs)
                for s in range(2):
                    t = it * 2 + s
                    cs.did(v.scalar_tensor_tensor(out=h1[:, s, :], in0=agg[:, ds(t * AW, D)], scalar=sm[:, s, 1:2],
                                                  in1=flat(work[:, ds(t, 1), :]), op0=ALU.mult, op1=ALU.add))
                sync(cs)
                norm_stats([h1[:, s, :] for s in range(2)])
                scaled([h1[:, s, :] for s in range(2)], V_G1)
                for s in range(2):
                    if not isinstance(it, int) or it > 0:
                        dve.wait_ge(c_x1T, it * 2 + (s - 1))
                        dve.wait_ge(c_x1b, it * 2 + (s - 1))
                    v.scalar_tensor_tensor(out=x1[:, s, :], in0=tmp[:, s, :], scalar=sm[:, s, 3:4],
                                           in1=vec[:, V_B1, :], op0=ALU.mult, op1=ALU.add).then_inc(c_x1, 1)
                dve.wait_ge(c_x1, it * 2 + 2)

            def other_norms(it):
                for s in range(2):
                    dve.wait_ge(c_f, it * 2 + (s + 1))
                    dve.wait_ge(c_x1b, it * 2 + (s + 1))
                    v.tensor_tensor(y1[:, s, :], flat(work[:, ds(it * 2 + s, 1), :]), bank(2 + s),
                                    ALU.add).then_inc(c_ft, 1)
                dve.wait_ge(c_ft, it * 2 + 2)
                ys_ = [y1[:, s, :] for s in range(2)]
                norm_stats(ys_)
                scaled(ys_, V_G2)
                for s in range(2):
                    cs.did(v.scalar_tensor_tensor(out=y1[:, s, :], in0=tmp[:, s, :], scalar=sm[:, s, 3:4],
                                                  in1=vec[:, V_B2, :], op0=ALU.mult, op1=ALU.add))
                sync(cs)
                for s in range(2):
                    cs.did(v.tensor_tensor(y1[:, s, :], y1[:, s, :], flat(x_res[:, ds(it * 2 + s, 1), :]), ALU.add))
                sync(cs)
                norm_stats(ys_)
                for s in range(2):
                    cs.did(v.tensor_scalar(flat(x_res[:, ds(it * 2 + s, 1), :]), y1[:, s, :], 1.0, None, ALU.mult))
                rsn.n += 2
                sync(rsn)
                for s in range(2):
                    v.tensor_scalar(xm[:, s, :], y1[:, s, :], mv[:, s, 0:1], sm[:, s, 3:4],
                                    ALU.subtract, ALU.mult).then_inc(c_xm, 1)
                for s in range(2):
                    cs.did(v.tensor_scalar(flat(work[:, ds(it * 2 + s, 1), :]), y1[:, s, :], mv[:, s, 0:1],
                                           sm[:, s, 3:4], ALU.subtract, ALU.mult))
                sync(cs)

            first_norm(0)
            first_norm(1)
            with dve.Fori(0, NT // 2 - 2) as it:
                cs.loop(it, 33)
                rsn.loop(it, 6)
                other_norms(it)
                first_norm(it + 2)
                dve.wait_ge(c_xmT, it * 2 + 2)
            cs.end(NT // 2 - 2)
            rsn.end(NT // 2 - 2)
            other_norms(NT // 2 - 2)
            dve.wait_ge(c_xmT, NT - 2)
            other_norms(NT // 2 - 1)

            rd = Steps(d_dve)

            def did(ins):
                rd.did(ins)
                sync(rd)

            per_t = [P, NT, EXPERTS]
            dve.wait_ge(c_lgt, NT)
            did(v.tensor_tensor(lg[:, :, :], lg[:, :, :], rb_s[:, :].unsqueeze(1).to_broadcast(per_t), ALU.add))
            did(v.tensor_reduce(var[:, :], lg[:, :, :], AX.X, ALU.max))
            v.tensor_tensor(lg[:, :, :], lg[:, :, :], var[:, :].unsqueeze(2).to_broadcast(per_t),
                            ALU.subtract).then_inc(d_lg0, 1)
            dve.wait_ge(d_ex, 1)
            did(v.tensor_reduce(var[:, :], lg[:, :, :], AX.X, ALU.add))
            did(v.reciprocal(rs[:, :], var[:, :]))
            did(v.tensor_tensor(probs, lg[:, :, :], rs[:, :].unsqueeze(2).to_broadcast(per_t), ALU.mult))
            for t in range(NT):
                rd.did(v.max(m8[:, t, :], probs[:, t, :]))
            sync(rd)
            for t in range(NT):
                rd.did(v.max_index(i8[:, t, :], m8[:, t, :], probs[:, t, :]))
            sync(rd)
            did(v.tensor_copy(idx_f[:, :, :], i8[:, :, 0:2]))
            for c, e in ((0, e1), (1, e2)):
                rd.did(v.tensor_tensor(e, num[:, 0:EXPERTS].unsqueeze(1).to_broadcast(per_t),
                                       idx_f[:, :, c:c + 1].to_broadcast(per_t), ALU.is_equal))
            sync(rd)
            v.tensor_tensor(oh_bf, flat(e1), flat(e2), ALU.add).then_inc(d_oh, 1)
            rd.did(v.tensor_tensor(gate_all, e1, m8[:, :, 0:1].to_broadcast(per_t), ALU.mult))
            rd.did(v.tensor_tensor(prod, e2, m8[:, :, 1:2].to_broadcast(per_t), ALU.mult))
            rd.did(v.memset(cum[:, 0, :], 0.0))
            sync(rd)
            v.tensor_tensor(gate_all, gate_all, prod, ALU.add).then_inc(d_gall, 1)
            dve.wait_ge(d_cnt, 1)
            for t in range(NT):
                did(v.tensor_tensor(cum[:, t + 1, :], cum[:, t, :], bank(1, t * EXPERTS, EXPERTS), ALU.add))
            did(v.tensor_scalar(cnt_i[:, :], cum[:, NT, :], float(P - 1), None, ALU.add))
            did(v.tensor_scalar(cnt_i[:, :], cnt_i[:, :], BLOCK_SHIFT, None, ALU.logical_shift_right))
            did(v.tensor_copy(row16[:, 0, :], cnt_i[:, :]))
            did(v.tensor_tensor_scan(row16[:, 1, :], ones[:, 0:EXPERTS], row16[:, 0, :], 0.0, ALU.mult, ALU.add))
            tab = [1, SLOT_TILES + 1, EXPERTS]
            did(v.tensor_tensor(tcmp[:, :, :], num[0:1, 0:SLOT_TILES + 1].unsqueeze(2).to_broadcast(tab),
                                row16[0:1, 1:2, :].to_broadcast(tab), ALU.is_ge))
            rd.did(v.tensor_copy(npair[0:1, 1:2], row16[0:1, 1, EXPERTS - 1:EXPERTS]))
            did(v.tensor_reduce(texp_f[:, :], tcmp[:, :, :], AX.X, ALU.add))
            v.tensor_scalar(texp[:, :], texp_f[:, :], float(EXPERTS - 1), None, ALU.min).then_inc(d_tab, 1)
            did(v.tensor_tensor(row16[:, 2, :], row16[:, 1, :], row16[:, 0, :], ALU.subtract))
            rd.did(v.tensor_scalar(row16[:, 3, :], row16[:, 2, :], float(P), None, ALU.mult))
            did(v.tensor_tensor(rank, cum[:, 0:NT, :], bank(0, 0, R).rearrange("p (t e) -> p t e", e=EXPERTS), ALU.add))
            did(v.tensor_tensor(rank, rank, row16[:, 3:4, :].to_broadcast(per_t), ALU.add))
            for c, e in ((0, e1), (1, e2)):
                did(v.tensor_tensor(prod, e, rank, ALU.mult))
                did(v.tensor_reduce(pos_f[:, :, c], prod, AX.X, ALU.add))
            v.tensor_copy(pos_i[:, :], flat(pos_f[:, :, :])).then_inc(d_pos, 1)
            for t in range(NT):
                dve.wait_ge(d_b2, t + 1)
                v.tensor_tensor(x_res[:, t, :], x_res[:, t, :], bank(4 + t % 4), ALU.add).then_inc(d_b2t, 1)

            def take(t, u):
                dve.wait_ge(e_y, t + 1)
                v.tensor_copy(ys[:, u, :], bank(3 + SCR[u])).then_inc(e_yt, 1)

            for u in range(MR):
                take(u, u)
            with dve.Fori(1, LOOPED) as it:
                for u in range(MR):
                    dve.wait_ge(e_out[u], it * 16)
                    take(it * MR + u, u)

            def take_rest(first, end):
                for t in range(first, end):
                    dve.wait_ge(e_out[t % MR], t // MR * 16)
                    take(t, t % MR)

            take_rest(LOOPED * MR, USUAL)
            with dve.If(tiles_used(dve) > USUAL):
                take_rest(USUAL, SLOT_TILES)

            dve.wait_ge(d_b2t, NT)
            for t in range(NT):
                dve.wait_ge(f_g[t % 4], 32 * (t // 4 + 1))
                v.scalar_tensor_tensor(out=x_res[:, t, :], in0=yg[:, t % 4, 0, :], scalar=m8[:, t, 0:1],
                                       in1=x_res[:, t, :], op0=ALU.mult, op1=ALU.add).then_inc(f_dve, 1)
                dve.wait_ge(f_dve, t + 1)
                v.scalar_tensor_tensor(out=x_res[:, t, :], in0=yg[:, t % 4, 1, :], scalar=m8[:, t, 1:2],
                                       in1=x_res[:, t, :], op0=ALU.mult, op1=ALU.add).then_inc(f_done, 1)


def kernel(**inputs):
    import numpy as np
    import concourse.bacc as bacc
    from concourse.bass_utils import run_bass_kernel_spmd

    a = {k: np.ascontiguousarray(v) for k, v in inputs.items()}

    def chunks(v, fill):
        full = np.full((ECP * P,), fill, v.dtype)
        full[0:EDGES] = v
        return np.ascontiguousarray(full.reshape(ECP, P).T)

    x = np.zeros((NP, D), a["x"].dtype)
    x[0:NODES] = a["x"]
    experts = np.concatenate([
        a["L0_ffn_w1"].reshape(EXPERTS, EF, KD, P).transpose(0, 3, 2, 1).reshape(EXPERTS, P, KD * EF),
        a["L0_ffn_w2"].reshape(EXPERTS, D, KE, P).transpose(0, 3, 2, 1).reshape(EXPERTS, P, KE * D),
        a["L0_ffn_b1"].reshape(EXPERTS, KE, P).transpose(0, 2, 1)], axis=2)
    vecs = np.concatenate([a["L0_gnn_b_self"][None], a["L0_gnn_b_rel"]]
                          + [a["L0_gnn_" + n][None] for n in ("ln1_g", "ln1_b", "ln2_g", "ln2_b", "b_ffn2")], axis=0)
    arrays = {
        "x": x, "src": chunks(a["src"], 0), "dst": chunks(a["dst"], NODES - 1), "typ": chunks(a["edge_type_4"], 0),
        "wgt": chunks(a["edge_weight"], 0), "w_self": a["L0_gnn_W_self"], "w_rel": a["L0_gnn_W_rel"], "vecs": vecs,
        "w1": a["L0_gnn_W_ffn1"], "w2": a["L0_gnn_W_ffn2"],
        "bf1": np.ascontiguousarray(a["L0_gnn_b_ffn1"].reshape(KF, P).T),
        "rwT": np.ascontiguousarray(a["L0_ffn_router_w"].T), "rb": a["L0_ffn_router_b"],
        "experts": np.ascontiguousarray(experts), "eb2": a["L0_ffn_b2"],
    }
    nc = bacc.Bacc("TRN2", target_bir_lowering=False, num_devices=1)
    args = [nc.dram_tensor(n, v.shape, mybir.dt.from_np(v.dtype), kind="ExternalInput").ap() for n, v in arrays.items()]
    out = nc.dram_tensor("out", (NP, D), F32, kind="ExternalOutput").ap()
    program(nc, *args, out)
    r = run_bass_kernel_spmd(nc, [arrays], core_ids=[0])
    return r.results[0]["out"][0:NODES]
```
